# Optimizing a Trainium2 kernel written in Bass

```python
import numpy as np
import jax
import jax.numpy as jnp

def _softmax(x, axis=-1):
    return jax.nn.softmax(x, axis=axis)

def _gelu(x):
    return jax.nn.gelu(x, approximate=True)

def _silu(x):
    return jax.nn.silu(x)

def _sigmoid(x):
    return jax.nn.sigmoid(x)

def _layernorm(x, axis=-1, eps=1e-05):
    m = jnp.mean(x, axis=axis, keepdims=True)
    v = jnp.var(x, axis=axis, keepdims=True)
    return (x - m) / jnp.sqrt(v + eps)

def _scatter_add(tgt, idx, src, axis=0):
    return tgt.at[idx].add(src)

def _segment_sum(src, seg, n):
    return jax.ops.segment_sum(src, seg, n)
kernel_name = 'mk_recurrent_d1_jaxref_r4_88aa77'

def setup_inputs(seed: int=0):
    np.random.seed(seed)
    _w = jnp.asarray

    def _L0_attn_setup():
        import jax, jax.numpy as jnp
        import numpy as np
        B, L, D = (2, 512, 256)
        H, HD = (16, 64)
        LD = 64
        key = jax.random.key(seed)
        ks = jax.random.split(key, 6)
        s = lambda fan_in: 1.0 / np.sqrt(fan_in)
        x_bld = jax.random.normal(ks[0], (B, L, D), dtype=jnp.float32)
        Wq = jax.random.normal(ks[1], (D, H, HD), dtype=jnp.float32) * s(D)
        Wkv_down = jax.random.normal(ks[2], (D, LD), dtype=jnp.float32) * s(D)
        Wk_up = jax.random.normal(ks[3], (LD, H, HD), dtype=jnp.float32) * s(LD)
        Wv_up = jax.random.normal(ks[4], (LD, H, HD), dtype=jnp.float32) * s(LD)
        Wout = jax.random.normal(ks[5], (H, HD, D), dtype=jnp.float32) * s(H * HD)
        return {'x_bld': x_bld, 'Wq': Wq, 'Wkv_down': Wkv_down, 'Wk_up': Wk_up, 'Wv_up': Wv_up, 'Wout': Wout}
    _L0_attn_in = _L0_attn_setup()

    def _L0_ffn_setup():
        import jax, jax.numpy as jnp
        import numpy as np
        DIM = 256
        DEPTH = 2
        HEADS = 8
        DIM_HEAD = 64
        WINDOW = 128
        INNER = HEADS * DIM_HEAD
        HID = int(DIM * 4 * 2 / 3)
        B, N = (2, 2048)
        QK_SCALE = 8.0

        def shift_token(t):
            t1, t2 = jnp.split(t, 2, axis=-1)
            t2 = jnp.pad(t2, ((0, 0), (1, 0), (0, 0)))[:, :-1]
            return jnp.concatenate([t1, t2], axis=-1)

        def l2norm(t):
            return t / jnp.clip(jnp.linalg.norm(t, axis=-1, keepdims=True), 1e-12)

        def rotate_half(x):
            x1, x2 = jnp.split(x, 2, axis=-1)
            return jnp.concatenate([-x2, x1], axis=-1)

        def rotary_xpos(q, k):
            n = q.shape[-2]
            half_idx = jnp.arange(0, DIM_HEAD, 2, dtype=jnp.float32)
            inv_freq = 1.0 / 10000.0 ** (half_idx / DIM_HEAD)
            t = jnp.arange(n, dtype=jnp.float32)
            freqs = t[:, None] * inv_freq[None, :]
            freqs = jnp.concatenate([freqs, freqs], axis=-1)
            base = (half_idx + 0.4 * DIM_HEAD) / (1.4 * DIM_HEAD)
            power = (t - n // 2) / float(WINDOW // 2)
            scale = base[None, :] ** power[:, None]
            scale = jnp.concatenate([scale, scale], axis=-1)
            cos, sin = (jnp.cos(freqs), jnp.sin(freqs))
            q = q * cos * scale + rotate_half(q) * sin * scale
            k = k * cos / scale + rotate_half(k) * sin / scale
            return (q, k)

        def local_attention(q, k, v):
            b, h, n, d = q.shape
            w = n // WINDOW
            bq = q.reshape(b, h, w, WINDOW, d) * QK_SCALE
            bk = k.reshape(b, h, w, WINDOW, d)
            bv = v.reshape(b, h, w, WINDOW, d)

            def look_around(t):
                p = jnp.pad(t, ((0, 0), (0, 0), (1, 0), (0, 0), (0, 0)))
                return jnp.concatenate([p[:, :, :w], p[:, :, 1:]], axis=3)
            bk, bv = (look_around(bk), look_around(bv))
            bt = jnp.arange(n).reshape(w, WINDOW)
            btp = jnp.pad(bt, ((1, 0), (0, 0)), constant_values=-1)
            btk = jnp.concatenate([btp[:w], btp[1:]], axis=1)
            sim = jnp.einsum('bhwid,bhwjd->bhwij', bq, bk)
            i = bt[:, :, None]
            j = btk[:, None, :]
            mask = (i < j) | (i > j + WINDOW) | (j == -1)
            sim = jnp.where(mask, -jnp.finfo(sim.dtype).max, sim)
            attn = jax.nn.softmax(sim, axis=-1)
            out = jnp.einsum('bhwij,bhwjd->bhwid', attn, bv)
            return out.reshape(b, h, n, d)

        def _layer(x, wqkv, qs, ksc, wo, lg, lb, w1, b1, w2, b2):
            b, n, _ = x.shape
            h = shift_token(x)
            qkv = h @ wqkv
            q, k, v = jnp.split(qkv, 3, axis=-1)
            to_heads = lambda t: t.reshape(b, n, HEADS, DIM_HEAD).transpose(0, 2, 1, 3)
            q, k, v = (to_heads(q), to_heads(k), to_heads(v))
            q = l2norm(q) * qs
            k = l2norm(k) * ksc
            q, k = rotary_xpos(q, k)
            o = local_attention(q, k, v)
            o = o.transpose(0, 2, 1, 3).reshape(b, n, INNER)
            x = x + o @ wo
            h = shift_token(x)
            mu = h.mean(-1, keepdims=True)
            var = h.var(-1, keepdims=True)
            h = (h - mu) / jnp.sqrt(var + 1e-05) * lg + lb
            h = h @ w1 + b1
            a, g = jnp.split(h, 2, axis=-1)
            h = a * jax.nn.gelu(g, approximate=False)
            x = x + h @ w2 + b2
            return x
        key = jax.random.key(seed)
        ks = jax.random.split(key, 6)
        return {'x': jax.random.normal(ks[0], (B, N, DIM), jnp.float32), 'wqkv': jax.random.normal(ks[1], (DEPTH, DIM, 3 * INNER), jnp.float32) * 0.02, 'q_scale': jnp.ones((DEPTH, DIM_HEAD), jnp.float32), 'k_scale': jnp.ones((DEPTH, DIM_HEAD), jnp.float32), 'wo': jax.random.normal(ks[2], (DEPTH, INNER, DIM), jnp.float32) * 0.02, 'ln_g': jnp.ones((DEPTH, DIM), jnp.float32), 'ln_b': jnp.zeros((DEPTH, DIM), jnp.float32), 'w1': jax.random.normal(ks[3], (DEPTH, DIM, 2 * HID), jnp.float32) * 0.02, 'b1': jnp.zeros((DEPTH, 2 * HID), jnp.float32), 'w2': jax.random.normal(ks[4], (DEPTH, HID, DIM), jnp.float32) * 0.02, 'b2': jnp.zeros((DEPTH, DIM), jnp.float32)}
    _L0_ffn_in = _L0_ffn_setup()
    _d = {'L0_attn_x_bld': _L0_attn_in['x_bld'], 'L0_attn_Wq': _L0_attn_in['Wq'], 'L0_attn_Wkv_down': _L0_attn_in['Wkv_down'], 'L0_attn_Wk_up': _L0_attn_in['Wk_up'], 'L0_attn_Wv_up': _L0_attn_in['Wv_up'], 'L0_attn_Wout': _L0_attn_in['Wout'], 'L0_ffn_wqkv': _L0_ffn_in['wqkv'], 'L0_ffn_q_scale': _L0_ffn_in['q_scale'], 'L0_ffn_k_scale': _L0_ffn_in['k_scale'], 'L0_ffn_wo': _L0_ffn_in['wo'], 'L0_ffn_ln_g': _L0_ffn_in['ln_g'], 'L0_ffn_ln_b': _L0_ffn_in['ln_b'], 'L0_ffn_w1': _L0_ffn_in['w1'], 'L0_ffn_b1': _L0_ffn_in['b1'], 'L0_ffn_w2': _L0_ffn_in['w2'], 'L0_ffn_b2': _L0_ffn_in['b2']}
    _x0 = _d['L0_attn_x_bld']
    _d['L0_attn_x_bld'] = jax.random.normal(jax.random.fold_in(jax.random.key(seed), 1), (4, 1024, 256), dtype=_x0.dtype)
    del _x0
    return _d

def reference(L0_attn_x_bld, L0_attn_Wq, L0_attn_Wkv_down, L0_attn_Wk_up, L0_attn_Wv_up, L0_attn_Wout, L0_ffn_wqkv, L0_ffn_q_scale, L0_ffn_k_scale, L0_ffn_wo, L0_ffn_ln_g, L0_ffn_ln_b, L0_ffn_w1, L0_ffn_b1, L0_ffn_w2, L0_ffn_b2):

    def _L0_attn_ref(x_bld, Wq, Wkv_down, Wk_up, Wv_up, Wout):
        import jax, jax.numpy as jnp
        import numpy as np
        B, L, D = (2, 512, 256)
        H, HD = (16, 64)
        LD = 64
        q_blhd = jnp.einsum('bld,dhk->blhk', x_bld, Wq)
        latent_bll = jnp.einsum('bld,dc->blc', x_bld, Wkv_down)
        k_blhd = jnp.einsum('blc,chk->blhk', latent_bll, Wk_up)
        v_blhd = jnp.einsum('blc,chk->blhk', latent_bll, Wv_up)
        attn = jnp.einsum('bqhd,bkhd->bhqk', q_blhd, k_blhd) / jnp.sqrt(jnp.asarray(HD, dtype=x_bld.dtype))
        l = x_bld.shape[1]
        mask = (jnp.arange(l)[None, :] <= jnp.arange(l)[:, None])[None, None]
        neg_inf = jnp.finfo(attn.dtype).min
        attn = jax.nn.softmax(jnp.where(mask, attn, neg_inf), axis=-1)
        y_blhd = jnp.einsum('bhqk,bkhd->bqhd', attn, v_blhd)
        return jnp.einsum('bqhd,hdo->bqo', y_blhd, Wout)

    def _L0_ffn_ref(x, wqkv, q_scale, k_scale, wo, ln_g, ln_b, w1, b1, w2, b2):
        import jax, jax.numpy as jnp
        import numpy as np
        DIM = 256
        DEPTH = 2
        HEADS = 8
        DIM_HEAD = 64
        WINDOW = 128
        INNER = HEADS * DIM_HEAD
        HID = int(DIM * 4 * 2 / 3)
        B, N = (2, 2048)
        QK_SCALE = 8.0

        def shift_token(t):
            t1, t2 = jnp.split(t, 2, axis=-1)
            t2 = jnp.pad(t2, ((0, 0), (1, 0), (0, 0)))[:, :-1]
            return jnp.concatenate([t1, t2], axis=-1)

        def l2norm(t):
            return t / jnp.clip(jnp.linalg.norm(t, axis=-1, keepdims=True), 1e-12)

        def rotate_half(x):
            x1, x2 = jnp.split(x, 2, axis=-1)
            return jnp.concatenate([-x2, x1], axis=-1)

        def rotary_xpos(q, k):
            n = q.shape[-2]
            half_idx = jnp.arange(0, DIM_HEAD, 2, dtype=jnp.float32)
            inv_freq = 1.0 / 10000.0 ** (half_idx / DIM_HEAD)
            t = jnp.arange(n, dtype=jnp.float32)
            freqs = t[:, None] * inv_freq[None, :]
            freqs = jnp.concatenate([freqs, freqs], axis=-1)
            base = (half_idx + 0.4 * DIM_HEAD) / (1.4 * DIM_HEAD)
            power = (t - n // 2) / float(WINDOW // 2)
            scale = base[None, :] ** power[:, None]
            scale = jnp.concatenate([scale, scale], axis=-1)
            cos, sin = (jnp.cos(freqs), jnp.sin(freqs))
            q = q * cos * scale + rotate_half(q) * sin * scale
            k = k * cos / scale + rotate_half(k) * sin / scale
            return (q, k)

        def local_attention(q, k, v):
            b, h, n, d = q.shape
            w = n // WINDOW
            bq = q.reshape(b, h, w, WINDOW, d) * QK_SCALE
            bk = k.reshape(b, h, w, WINDOW, d)
            bv = v.reshape(b, h, w, WINDOW, d)

            def look_around(t):
                p = jnp.pad(t, ((0, 0), (0, 0), (1, 0), (0, 0), (0, 0)))
                return jnp.concatenate([p[:, :, :w], p[:, :, 1:]], axis=3)
            bk, bv = (look_around(bk), look_around(bv))
            bt = jnp.arange(n).reshape(w, WINDOW)
            btp = jnp.pad(bt, ((1, 0), (0, 0)), constant_values=-1)
            btk = jnp.concatenate([btp[:w], btp[1:]], axis=1)
            sim = jnp.einsum('bhwid,bhwjd->bhwij', bq, bk)
            i = bt[:, :, None]
            j = btk[:, None, :]
            mask = (i < j) | (i > j + WINDOW) | (j == -1)
            sim = jnp.where(mask, -jnp.finfo(sim.dtype).max, sim)
            attn = jax.nn.softmax(sim, axis=-1)
            out = jnp.einsum('bhwij,bhwjd->bhwid', attn, bv)
            return out.reshape(b, h, n, d)

        def _layer(x, wqkv, qs, ksc, wo, lg, lb, w1, b1, w2, b2):
            b, n, _ = x.shape
            h = shift_token(x)
            qkv = h @ wqkv
            q, k, v = jnp.split(qkv, 3, axis=-1)
            to_heads = lambda t: t.reshape(b, n, HEADS, DIM_HEAD).transpose(0, 2, 1, 3)
            q, k, v = (to_heads(q), to_heads(k), to_heads(v))
            q = l2norm(q) * qs
            k = l2norm(k) * ksc
            q, k = rotary_xpos(q, k)
            o = local_attention(q, k, v)
            o = o.transpose(0, 2, 1, 3).reshape(b, n, INNER)
            x = x + o @ wo
            h = shift_token(x)
            mu = h.mean(-1, keepdims=True)
            var = h.var(-1, keepdims=True)
            h = (h - mu) / jnp.sqrt(var + 1e-05) * lg + lb
            h = h @ w1 + b1
            a, g = jnp.split(h, 2, axis=-1)
            h = a * jax.nn.gelu(g, approximate=False)
            x = x + h @ w2 + b2
            return x
        for l in range(DEPTH):
            x = _layer(x, wqkv[l], q_scale[l], k_scale[l], wo[l], ln_g[l], ln_b[l], w1[l], b1[l], w2[l], b2[l])
        return x
    x = L0_attn_x_bld
    xn = _layernorm(x, axis=-1)
    s = _L0_attn_ref(xn, L0_attn_Wq, L0_attn_Wkv_down, L0_attn_Wk_up, L0_attn_Wv_up, L0_attn_Wout)
    g = _silu(_L0_ffn_ref(xn, L0_ffn_wqkv, L0_ffn_q_scale, L0_ffn_k_scale, L0_ffn_wo, L0_ffn_ln_g, L0_ffn_ln_b, L0_ffn_w1, L0_ffn_b1, L0_ffn_w2, L0_ffn_b2))
    x = x + s * g
    return x

_drawn_inputs = setup_inputs


def setup_inputs(seed=0):
    import zlib

    import numpy as np

    out = dict(_drawn_inputs(seed))
    spreads = {'L0_ffn_q_scale': (1.0, 0.6),
     'L0_ffn_k_scale': (1.0, 0.6),
     'L0_ffn_ln_g': (1.0, 0.6),
     'L0_ffn_ln_b': (0.0, 0.8),
     'L0_ffn_b1': (0.0, 0.8),
     'L0_ffn_b2': (0.0, 2.0)}
    factors = {'L0_ffn_wqkv': 8.0, 'L0_ffn_wo': 8.0, 'L0_ffn_w1': 8.0, 'L0_ffn_w2': 8.0}
    for name, (base, spread) in spreads.items():
        noise = np.random.default_rng([zlib.crc32(name.encode()), seed]).standard_normal(out[name].shape)
        drawn = base * np.exp(spread * noise) if base else spread * noise
        out[name] = jnp.asarray(drawn.astype(out[name].dtype))
    for name, factor in factors.items():
        out[name] = (out[name] * factor).astype(out[name].dtype)
    return out
```

```python
from contextlib import ExitStack

import numpy as np

import concourse.bass as bass
from concourse import mybir

F32 = mybir.dt.float32
F32R = mybir.dt.float32r
ALU = mybir.AluOpType
ACT = mybir.ActivationFunctionType
AX_X = mybir.AxisListType.X

P = 128
B, N, D = 4, 1024, 256
KD = D // P
NT = N // P
CH = 512
NC = N // CH
TC = CH // P
DH = 64
LH = 8
LP = LH // 2
INNER = LH * DH
DEPTH = 2
HID = 682
HT = -(-HID // P)
HW = -(-HID // HT)
HREM = HID - (HT - 1) * HW
GH = 16
GP = GH // 2
EPS = 1e-5
NEG = -1e30
BIG = 3e38
SLOTS = 5


def rows_of(j):
    return HW if j < HT - 1 else HREM


def rotary_tables():
    f = np.float32
    half = np.arange(0, DH, 2, dtype=f)
    inv = (f(1.0) / np.power(f(10000.0), half / f(DH))).astype(f)
    t = np.arange(N, dtype=f)
    freqs = (t[:, None] * inv[None, :]).astype(f)
    base = ((half + f(0.4 * DH)) / f(1.4 * DH)).astype(f)
    power = ((t - f(N // 2)) / f(64.0)).astype(f)
    scale = np.power(base[None, :], power[:, None]).astype(f)
    cos, sin = np.cos(freqs).astype(f), np.sin(freqs).astype(f)
    six = np.stack([cos * scale, -sin * scale, sin * scale, cos / scale, -sin / scale, sin / scale], 1)
    return np.ascontiguousarray(six.reshape(NT, P, 6, DH // 2).transpose(1, 0, 2, 3).astype(f))


def semaphores(nc, ctx, prefix, names):
    return {n: ctx.enter_context(nc.semaphore(prefix + n)) for n in names.split()}


def clear(nc, sems):
    with nc.Block() as block:
        @block.gpsimd
        def _(pool):
            for sem in sems.values():
                pool.sem_clear(sem)


def three(pe, out, pairs, start=True, stop=True):
    last, n = None, len(pairs)
    for i, (wh, wl, xh, xl) in enumerate(pairs):
        pe.matmul(out, wh, xh, start=start and i == 0, stop=False)
        pe.matmul(out, wh, xl, start=False, stop=False)
        last = pe.matmul(out, wl, xh, start=False, stop=stop and i == n - 1)
    return last


def setup(nc, ident, ones, eps, s):
    with nc.Block() as block:
        @block.gpsimd
        def _(pool):
            pool.memset(ident[:, :], 0.0).then_inc(s["const"], 1)
            pool.memset(ones[:, :], 1.0 / D).then_inc(s["const"], 1)
            pool.memset(eps[:, :], EPS).then_inc(s["const"], 1)
            pool.wait_ge(s["const"], 3)
            pool.affine_select(out=ident[:, :], in_=ident[:, :], compare_op=ALU.not_equal, fill=1.0,
                               base=0, pattern=[[-1, P]], channel_multiplier=1).then_inc(s["const"], 1)
            pool.wait_ge(s["const"], 4)
    clear(nc, s)


def layernorm_tokens(dve, s, xtok, xn, bst, mv, dev, rstd):
    dve.wait_ge(s["x_in"], 16)
    for t in range(NT):
        dve.bn_stats(bst[:, t, :], xtok[:, t, :]).then_inc(s["stats"], 1)
    for t in range(NT):
        dve.wait_ge(s["stats"], t + 1)
        dve.bn_aggr(mv[:, t, :], bst[:, t, :]).then_inc(s["moments"], 1)
    dve.wait_ge(s["dev"], 1)
    dve.reciprocal(rstd[:, :], dev[:, :]).then_inc(s["rstd"], 1)
    dve.wait_ge(s["rstd"], 1)
    for t in range(NT):
        dve.tensor_scalar(xn[:, t, :], xtok[:, t, :], mv[:, t, 0:1], rstd[:, t:t + 1],
                          ALU.subtract, ALU.mult).then_inc(s["xn"], 1)


def deviations(act, s, mv, dev, eps):
    act.wait_ge(s["moments"], NT)
    act.activation(dev[:, :], mv[:, :, 1], ACT.Sqrt, bias=eps[:, :]).then_inc(s["dev"], 1)


def transpose_tokens(pe, s, xn, ps, ident):
    for kt in range(KD):
        for c in range(NC):
            for t in range(TC):
                g = c * TC + t
                pe.wait_ge(s["xn"], g + 1)
                last = pe.transpose(ps[:, kt * NC + c, t * P:(t + 1) * P], xn[:, g, kt * P:(kt + 1) * P],
                                    ident[:, :])
            last.then_inc(s["xnT"], 1)


def stage_n(nc, x, state, ident, eps, ps):
    with ExitStack() as ctx:
        sb = lambda n, sh, dt=F32: ctx.enter_context(nc.sbuf_tensor(n, sh, dt))
        s = semaphores(nc, ctx, "n_", "x_in stats moments dev rstd xn xnT copied out")
        xtok = sb("n_xtok", [P, NT, D])
        xn = sb("n_xn", [P, NT, D])
        xT = sb("n_xT", [P, KD, N])
        bst = sb("n_bst", [P, NT, 6])
        mv = sb("n_mv", [P, NT, 2])
        dev = sb("n_dev", [P, NT])
        rstd = sb("n_rstd", [P, NT])
        with nc.Fori(0, B) as b:
            with nc.Block() as block:
                @block.sync
                def _(sp):
                    sp.dma_start(xtok[:, :, :], x[bass.ds(b, 1)].rearrange("b (t p) d -> p (b t) d", p=P)
                                 ).then_inc(s["x_in"], 16)
                    sp.wait_ge(s["copied"], KD * NC)
                    sp.dma_start(state[bass.ds(b, 1)].rearrange("b p k n -> p (b k) n"), xT[:, :, :]
                                 ).then_inc(s["out"], 16)
                    sp.wait_ge(s["out"], 16)

                @block.vector
                def _(dve):
                    layernorm_tokens(dve, s, xtok, xn, bst, mv, dev, rstd)

                @block.tensor
                def _(pe):
                    transpose_tokens(pe, s, xn, ps, ident)

                @block.scalar
                def _(act):
                    deviations(act, s, mv, dev, eps)
                    for i in range(KD * NC):
                        act.wait_ge(s["xnT"], i + 1)
                        act.activation(xT[:, i // NC, (i % NC) * CH:(i % NC + 1) * CH], ps[:, i, :],
                                       ACT.Copy).then_inc(s["copied"], 1)
            clear(nc, s)


def stage_l(nc, A, state, ident, ones, eps, ps):
    (wqkv, q_scale, k_scale, wo, ln_g, ln_b, w1, b1, w2, b2, rot) = A
    with ExitStack() as ctx:
        sb = lambda n, sh, dt=F32: ctx.enter_context(nc.sbuf_tensor(n, sh, dt))
        two = lambda n, sh: (sb(n + "_hi", sh, F32R), sb(n + "_lo", sh, F32R))
        Wq_hi, Wq_lo = two("l_wqkv", [P, KD, 3 * INNER])
        W1_hi, W1_lo = two("l_w1", [P, KD, 2 * HID])
        W2_hi, W2_lo = two("l_w2", [P, HT, D])
        Wo_hi, Wo_lo = two("l_wo", [P, LP, D])
        b1c = sb("l_b1", [P, 2, HT])
        b2c = sb("l_b2", [P, KD])
        lg = sb("l_lg", [P, KD])
        lb = sb("l_lb", [P, KD])
        qsc = sb("l_qsc", [P, 2, DH])
        rotC = sb("l_rotC", [P, 2, NT, DH])
        rotS = sb("l_rotS", [P, 2, NT, DH])
        mask = sb("l_mask", [P, 3 * P])
        xw = sb("l_xw", [P, KD, N + 1])
        xout = sb("l_xout", [P, KD, CH])
        xsave = sb("l_xsave", [P, 1])
        xh, xl = two("l_x", [P, KD, CH])
        hh_, hl_ = two("l_h", [P, KD, CH])
        ah, al = two("l_act", [P, HT, CH])
        qT = sb("l_qT", [P, LP, CH])
        kT = sb("l_kT", [P, LP, 2, SLOTS * P])
        vv = sb("l_v", [P, SLOTS, INNER])
        sq = sb("l_sq", [P, 2 * CH])
        t1 = sb("l_t1", [P, 2, 2, INNER])
        t2 = sb("l_t2", [P, 2, INNER])
        kn = sb("l_kn", [P, INNER])              
        ssq = sb("l_ssq", [P, 2, 2 * LH])
        norm = sb("l_norm", [P, 2, 2 * LH])
        rn = sb("l_rn", [P, 2, 2 * LH])
        hdev = sb("l_hdev", [P, 2, TC])
        hrs = sb("l_hrs", [P, 2, TC])
        nrn = sb("l_nrn", [P, NT, LH])
        SP = sb("l_sp", [P, 4, 2, 2 * P])
        mn = sb("l_mn", [P, 4, 2])
        ls = sb("l_ls", [P, 2, LH])
        rl = sb("l_rl", [P, 2, LH])
        PT = sb("l_pt", [P, 3, CH])
        rbs = sb("l_rbs", [P, 2, CH])
        ctxf = sb("l_ctxf", [P, 2, CH])
        assert LP * P == CH

        w = semaphores(nc, ctx, "lw_", "load mask masked tab bias biased scaled hi lo zero")
        s = semaphores(nc, ctx, "l_", "x_in x_hi x_lo x_saved qkv sq v ssq rn qrot krot qadd kadd tq tk "
                 "qT clamp norm hdev rsb kTa kTd sc ttr ex tr evd eva pv rl rb rbs ctx chi clo "
                 "wo xw mean hc hsq var rs hn hhi hlo ag ge u uhi ulo w2 xout out knorm nrn")

        kflat = kT[:, :, :, :].rearrange("p a b c -> p (a b c)")
        vflat = vv[:, :, :].rearrange("p a b -> p (a b)")
        qflat = qT[:, :, :].rearrange("p a b -> p (a b)")
        st_q = kflat[:, 0:KD * 3 * INNER].rearrange("p (k n) -> p k n", k=KD)
        st_1 = [kflat[:, KD * 3 * INNER:KD * 3 * INNER + 2 * HID], qflat[:, 0:2 * HID]]
        st_o = vflat[:, 0:LP * D].rearrange("p (k n) -> p k n", k=LP)
        st_2 = vflat[:, LP * D:(LP + HT) * D].rearrange("p (k n) -> p k n", k=HT)
        NR = NT * 6 * (DH // 2)
        st_r = xw[:, :, :].rearrange("p a b -> p (a b)")[:, 0:NR].rearrange("p (t s f) -> p t s f", t=NT, s=6)
        LOADS = 16

        def layer_block(block, b):
            UC = TC * LP
            H2 = DH // 2
            BQ, BK, BV = 0, 1, 2
            BTQ, BTK = 6, 7
            BS = 0
            BP = 3
            BC = 5
            BR = 7

            heads = lambda ap: ap.rearrange("p (h d) -> p h d", h=LH)
            halves = lambda ap: ap.rearrange("p (h a f) -> p h a f", h=LH, a=2)
            chunk = lambda c: slice(c * CH, (c + 1) * CH)
            hcen = t2

            def keys(u):
                g = u // LP
                if g == 0:
                    return [0], mask[:, P:2 * P]
                a, c = (g - 1) % SLOTS, g % SLOTS
                return ([a, c], mask[:, 0:2 * P]) if a < c else ([c, a], mask[:, P:3 * P])

            def copy_turned(eng, u):
                slots, _ = keys(u)
                k = len(slots) * P
                src = ps[:, BP + u % 2, :].rearrange("p (h k) -> p h k", h=2)[:, :, 0:k]
                dst = PT[:, u % 3, :].rearrange("p (h k) -> p h k", h=2)[:, :, 0:k]
                if u % 2:
                    return eng.activation(dst, src, ACT.Copy)
                return eng.tensor_copy(dst, src)

            @block.sync
            def _(sp):
                sp.dma_start(xw[:, :, 1:N + 1], state[bass.ds(b, 1)].rearrange("b p k n -> p (b k) n")
                             ).then_inc(s["x_in"], 16)
                for c in range(NC):
                    sp.wait_ge(s["xout"], KD * (c + 1))
                    sp.dma_start(state[bass.ds(b, 1), :, :, chunk(c)].rearrange("b p k n -> p (b k) n"), xout[:, :, :]
                                 ).then_inc(s["out"], 16)
                sp.wait_ge(s["out"], 16 * NC)

            @block.tensor
            def _(pe):
                def qkv(g):
                    c, t = g // TC, g % TC
                    if t == 0:
                        pe.wait_ge(s["x_lo"], KD if c == 0 else 2 * KD + 1)
                        if c:
                            pe.wait_ge(s["xout"], KD * c)
                            pe.wait_ge(s["u"], HT * c)
                    if t >= 2:
                        pe.wait_ge(s["krot"], g - 1)
                        pe.wait_ge(s["v"], g - 1)
                    for i in range(3):
                        cols = slice(i * INNER, (i + 1) * INNER)
                        tok = slice(t * P, (t + 1) * P)
                        three(pe, ps[:, 3 * (t % 2) + i, :],
                              [(xh[:, k, tok], xl[:, k, tok], Wq_hi[:, k, cols], Wq_lo[:, k, cols]) for k in range(KD)]
                              ).then_inc(s["qkv"], 1)

                def turn(g):
                    pe.wait_ge(s["qadd"], g + 1)
                    if g:
                        pe.wait_ge(s["qT"], g)
                        pe.wait_ge(s["kTa"], g)
                        pe.wait_ge(s["kTd"], g)
                    if g == TC:
                        pe.wait_ge(s["u"], HT)
                    for j in range(LP):
                        last = pe.transpose(ps[:, BTQ, j * P:(j + 1) * P], t1[:, g % 2, 0, j * P:(j + 1) * P], ident[:, :])
                    last.then_inc(s["tq"], 1)
                    pe.wait_ge(s["kadd"], g + 1)
                    for j in range(LP):
                        last = pe.transpose(ps[:, BTK, j * P:(j + 1) * P], t1[:, g % 2, 1, j * P:(j + 1) * P], ident[:, :])
                    last.then_inc(s["tk"], 1)

                def scores(u):
                    j, g = u % LP, u // LP
                    if u % UC == 0:
                        pe.wait_ge(s["qT"], g + TC)
                        pe.wait_ge(s["kTa"], g + TC)
                        pe.wait_ge(s["kTd"], g + TC)
                        pe.wait_ge(s["krot"], g + TC)
                        pe.wait_ge(s["v"], g + TC)
                    if u % UC >= 3:
                        pe.wait_ge(s["ttr"], 2 * (u - 2))
                    slots, _ = keys(u)
                    n = P * len(slots)
                    kview = kT[:, j, :, :].rearrange("p h (s k) -> p h s k", s=SLOTS)
                    a = slots[0]
                    if len(slots) == 1:
                        rhs = kview[:, :, a, :]
                    else:
                        rhs = kview[:, :, a:slots[1] + 1:slots[1] - a, :]
                    out = ps[:, BS + u % 3, 0:2 * n]
                    t = g % TC
                    pe.matmul(out, qT[:, j, t * P:(t + 1) * P], rhs, start=True, stop=True).then_inc(s["sc"], 1)

                def turn_p(u):
                    pe.wait_ge(s["ex"], 2 * (u + 1))
                    if u % UC >= 2:
                        pe.wait_ge(s["eva"] if u % 2 else s["evd"], u // 2)
                    slots, _ = keys(u)
                    for h in range(2):
                        for i in range(len(slots)):
                            k = h * 2 + i
                            last = pe.transpose(ps[:, BP + u % 2, k * P:(k + 1) * P], SP[:, u % 4, h, i * P:(i + 1) * P],
                                                ident[:, :])
                    last.then_inc(s["tr"], 1)

                def weigh(u):
                    j, g = u % LP, u // LP
                    pe.wait_ge(s["eva"] if u % 2 else s["evd"], u // 2 + 1)
                    if j == 0 and g >= 2:
                        pe.wait_ge(s["ctx"], g - 1)
                    slots, _ = keys(u)
                    for i, sl in enumerate(slots):
                        for h in range(2):
                            last = pe.matmul(ps[64 * h:64 * h + 64, BC + g % 2, j * P:(j + 1) * P],
                                             vv[:, sl, (2 * j + h) * DH:(2 * j + h + 1) * DH],
                                             PT[:, u % 3, (2 * h + i) * P:(2 * h + i + 1) * P],
                                             start=(i == 0), stop=(i == len(slots) - 1), skip_group_check=True)
                    last.then_inc(s["pv"], 1)

                def spread(g):
                    pe.wait_ge(s["rl"], g + 1)
                    if g % TC:
                        pe.wait_ge(s["rbs"], g)
                    for j in range(LP):
                        for h in range(2):
                            last = pe.matmul(ps[64 * h:64 * h + 64, BR, j * P:(j + 1) * P],
                                             rl[:, g % 2, 2 * j + h:2 * j + h + 1].to_broadcast([P, DH]), ident[:, :],
                                             start=True, stop=True, skip_group_check=True)
                    last.then_inc(s["rb"], 1)

                def project(c):
                    pe.wait_ge(s["clo"], TC * (c + 1))
                    pe.wait_ge(s["ttr"], 2 * UC * (c + 1))
                    for m_ in range(KD):
                        f = slice(m_ * P, (m_ + 1) * P)
                        three(pe, ps[:, m_, :], [(Wo_hi[:, k, f], Wo_lo[:, k, f], ah[:, k, :], al[:, k, :])
                                                 for k in range(LP)]).then_inc(s["wo"], 1)

                def feed(c):
                    pe.wait_ge(s["xw"], KD * (c + 1))
                    for k, rhs in enumerate((xw[:, 0, 1 + c * CH:1 + (c + 1) * CH], xw[:, 1, chunk(c)])):
                        last = pe.matmul(ps[:, 2, :], ones[:, :], rhs, start=(k == 0), stop=(k == KD - 1))
                    last.then_inc(s["mean"], 1)
                    pe.wait_ge(s["hsq"], c + 1)
                    for t in range(TC):
                        for k in range(KD):
                            last = pe.matmul(ps[:, 3, t:t + 1], sq[:, k * CH + t * P:k * CH + (t + 1) * P],
                                             ones[:, 0:1], start=(k == 0), stop=(k == KD - 1))
                    last.then_inc(s["var"], 1)
                    pe.wait_ge(s["rs"], c + 1)
                    for t in range(TC):
                        last = pe.transpose(ps[:, 2, t * P:(t + 1) * P], hrs[:, c, t:t + 1].to_broadcast([P, P]),
                                            ident[:, :])
                    last.then_inc(s["rsb"], 1)
                    pe.wait_ge(s["hlo"], c + 1)
                    pe.wait_ge(s["eva"], UC // 2 * (c + 1))
                    pe.wait_ge(s["ctx"], TC * (c + 1))

                    def up(j):
                        n, mj = HT * c + j, rows_of(j)
                        if j >= 2:
                            pe.wait_ge(s["u"], n - 1)
                        for i in (1, 0):
                            f = slice(i * HID + j * HW, i * HID + j * HW + mj)
                            three(pe, ps[0:mj, 4 + 2 * (j % 2) + i, :],
                                  [(W1_hi[:, k, f], W1_lo[:, k, f], hh_[:, k, :], hl_[:, k, :]) for k in range(KD)]
                                  ).then_inc(s["ag"], 1)

                    def down(j):
                        n, mj = HT * c + j, rows_of(j)
                        pe.wait_ge(s["ulo"], n + 1)
                        for m_ in range(KD):
                            f = slice(m_ * P, (m_ + 1) * P)
                            last = three(pe, ps[:, m_, :], [(W2_hi[0:mj, j, f], W2_lo[0:mj, j, f], ah[0:mj, j, :],
                                                             al[0:mj, j, :])], start=(j == 0), stop=(j == HT - 1))
                            if j == HT - 1:
                                last.then_inc(s["w2"], 1)

                    for j in range(HT + 2):
                        if j < HT:
                            up(j)
                        if j >= 2:
                            down(j - 2)

                for c in range(NC):
                    for t in range(TC + 1):
                        if t < TC:
                            qkv(c * TC + t)
                        if t >= 1:
                            turn(c * TC + t - 1)
                    for i in range(UC + 4):
                        u = c * UC + i
                        if i < UC:
                            scores(u)
                        if 2 <= i < UC + 2:
                            turn_p(u - 2)
                        if 3 <= i < UC + 3:
                            weigh(u - 3)
                        if i >= 7 and (i - 7) % LP == 0:
                            spread((u - 7) // LP)
                    project(c)
                    feed(c)

            @block.scalar
            def _(act):
                def tile_a(g):
                    pr = 3 * (g % TC % 2)
                    act.wait_ge(s["qkv"], 3 * g + 1)
                    if g:
                        act.wait_ge(s["ssq"], g)
                    if g == TC:
                        act.wait_ge(s["var"], 1)
                    act.activation(sq[:, 0:CH], ps[:, pr + BQ, :], ACT.Square).then_inc(s["sq"], 1)
                    act.wait_ge(s["qkv"], 3 * g + 2)
                    act.activation(sq[:, CH:2 * CH], ps[:, pr + BK, :], ACT.Square).then_inc(s["sq"], 1)
                    act.wait_ge(s["qkv"], 3 * g + 3)
                    if g >= SLOTS:
                        act.wait_ge(s["pv"], LP * (g - SLOTS + 2))
                    act.activation(vv[:, g % SLOTS, :], ps[:, pr + BV, :], ACT.Copy).then_inc(s["v"], 1)
                    act.wait_ge(s["clamp"], g + 1)
                    act.activation(norm[:, g % 2, :], ssq[:, g % 2, :], ACT.Sqrt).then_inc(s["norm"], 1)

                def tile_t(g):
                    act.wait_ge(s["tq"], g + 1)
                    t = g % TC
                    if g >= TC and t == 0:
                        act.wait_ge(s["sc"], UC)
                    act.activation(qT[:, :, t * P:(t + 1) * P], ps[:, BTQ, :].rearrange("p (j k) -> p j k", j=LP),
                                   ACT.Copy).then_inc(s["qT"], 1)
                    act.wait_ge(s["tk"], g + 1)
                    sl = g % SLOTS
                    act.activation(kT[0:64, :, 0, sl * P:(sl + 1) * P],
                                   ps[0:64, BTK, :].rearrange("p (j k) -> p j k", j=LP), ACT.Copy).then_inc(s["kTa"], 1)

                def exps(u):
                    j, g = u % LP, u // LP
                    slots, _ = keys(u)
                    n = P * len(slots)
                    if j == 0 and g >= 2:
                        act.wait_ge(s["rl"], g - 1)
                    for h in range(2):
                        act.wait_ge(s["ttr"], 2 * u + h + 1)
                        act.activation(SP[:, u % 4, h, 0:n], SP[:, u % 4, h, 0:n], ACT.Exp, bias=mn[:, u % 4, h:h + 1],
                                       scale=-1.0, accum_out=ls[:, g % 2, 2 * j + h:2 * j + h + 1]).then_inc(s["ex"], 1)

                def copy_p(u):
                    act.wait_ge(s["tr"], u + 1)
                    if u >= 3:
                        act.wait_ge(s["pv"], u - 2)
                    copy_turned(act, u).then_inc(s["eva"], 1)

                def copy_r(g):
                    act.wait_ge(s["rb"], g + 1)
                    if g >= 2:
                        act.wait_ge(s["ctx"], g - 1)
                    act.activation(rbs[:, g % 2, :], ps[:, BR, :], ACT.Copy).then_inc(s["rbs"], 1)

                for c in range(NC):
                    for t in range(TC + 1):
                        if t < TC:
                            tile_a(c * TC + t)
                        if t >= 1:
                            tile_t(c * TC + t - 1)
                    for i in range(UC + 4):
                        u = c * UC + i
                        if i < UC:
                            exps(u)
                        if 2 <= i < UC + 2 and (i - 2) % 2:
                            copy_p(u - 2)
                        if i >= 7 and (i - 7) % LP == 0:
                            copy_r((u - 7) // LP)
                    act.wait_ge(s["hc"], KD * (c + 1))
                    act.activation(sq[:, :], hcen[:, :, :].rearrange("p a b -> p (a b)"), ACT.Square).then_inc(s["hsq"], 1)
                    act.wait_ge(s["var"], c + 1)
                    act.activation(hdev[:, c, :], ps[:, 3, 0:TC], ACT.Sqrt, bias=eps[:, :]).then_inc(s["hdev"], 1)
                    for j in range(HT):
                        n, mj = HT * c + j, rows_of(j)
                        act.wait_ge(s["ag"], 2 * n + 1)
                        if j >= 2:
                            act.wait_ge(s["u"], n - 1)
                        act.activation(rbs[0:mj, j % 2, :], ps[0:mj, 4 + 2 * (j % 2) + 1, :], ACT.Gelu,
                                       bias=b1c[0:mj, 1, j:j + 1]).then_inc(s["ge"], 1)

            @block.vector
            def _(dve):
                def split(c):
                    if c == 0:
                        dve.wait_ge(s["x_in"], 16)
                        dve.tensor_copy(xsave[:, :], xw[:, 1, CH:CH + 1]).then_inc(s["x_saved"], 1)
                    else:
                        dve.wait_ge(s["qkv"], 3 * TC * c)
                    own, prev = xw[:, 0, 1 + c * CH:1 + (c + 1) * CH], xw[:, 1, chunk(c)]
                    dve.tensor_copy(xh[:, 0, :], own).then_inc(s["x_hi"], 1)
                    if c == 0:
                        dve.tensor_copy(xh[:, 1, :], prev).then_inc(s["x_hi"], 1)
                        dve.wait_ge(s["x_hi"], 2)
                        dve.tensor_tensor(xl[:, 0, :], own, xh[:, 0, :], ALU.subtract).then_inc(s["x_lo"], 1)
                        dve.tensor_tensor(xl[:, 1, :], prev, xh[:, 1, :], ALU.subtract).then_inc(s["x_lo"], 1)
                    else:
                        dve.wait_ge(s["x_saved"], 1)
                        dve.tensor_copy(xh[:, 1, 0:1], xsave[:, :]).then_inc(s["x_hi"], 1)
                        dve.tensor_copy(xh[:, 1, 1:CH], xw[:, 1, c * CH + 1:(c + 1) * CH]).then_inc(s["x_hi"], 1)
                        dve.wait_ge(s["x_hi"], 5)
                        dve.tensor_tensor(xl[:, 0, :], own, xh[:, 0, :], ALU.subtract).then_inc(s["x_lo"], 1)
                        dve.tensor_tensor(xl[:, 1, 1:CH], xw[:, 1, c * CH + 1:(c + 1) * CH], xh[:, 1, 1:CH],
                                          ALU.subtract).then_inc(s["x_lo"], 1)
                        dve.tensor_tensor(xl[:, 1, 0:1], xsave[:, :], xh[:, 1, 0:1], ALU.subtract).then_inc(s["x_lo"], 1)

                def tile_a(g):
                    pr = 3 * (g % TC % 2)
                    q, k = ps[:, pr + BQ, :], ps[:, pr + BK, :]
                    dve.wait_ge(s["sq"], 2 * g + 2)
                    dve.tensor_reduce(ssq[:, g % 2, :], sq[:, :].rearrange("p (h d) -> p h d", d=DH), AX_X,
                                      ALU.add).then_inc(s["ssq"], 1)
                    dve.wait_ge(s["ssq"], g + 1)
                    dve.tensor_scalar(ssq[:, g % 2, :], ssq[:, g % 2, :], 1e-24, None, ALU.max).then_inc(s["clamp"], 1)
                    C = lambda i: rotC[:, i, g:g + 1, :].to_broadcast([P, LH, DH])
                    S = lambda i, a: rotS[:, i, g:g + 1, a * H2:(a + 1) * H2].to_broadcast([P, LH, H2])
                    if g >= 2:
                        dve.wait_ge(s["tk"], g - 1)
                    dve.tensor_tensor(heads(t1[:, g % 2, 0, :]), heads(q), C(0), ALU.mult).then_inc(s["qrot"], 1)
                    if g:
                        dve.wait_ge(s["qadd"], g)
                    for a in range(2):
                        dve.tensor_tensor(halves(t2[:, 0, :])[:, :, a, :], halves(q)[:, :, 1 - a, :], S(0, a),
                                          ALU.mult).then_inc(s["qrot"], 1)
                    dve.wait_ge(s["norm"], g + 1)
                    dve.reciprocal(rn[:, g % 2, :], norm[:, g % 2, :]).then_inc(s["rn"], 1)
                    dve.wait_ge(s["rn"], g + 1)
                    dve.tensor_scalar(nrn[:, g, :], rn[:, g % 2, 0:LH], -8.0, None, ALU.mult).then_inc(s["nrn"], 1)
                    dve.tensor_tensor(heads(kn[:, :]), heads(k), rn[:, g % 2, LH:2 * LH].unsqueeze(2).to_broadcast(
                        [P, LH, DH]), ALU.mult).then_inc(s["krot"], 1)
                    dve.wait_ge(s["krot"], g + 1)
                    dve.tensor_tensor(heads(t1[:, g % 2, 1, :]), heads(kn[:, :]), C(1), ALU.mult).then_inc(s["knorm"], 1)
                    if g:
                        dve.wait_ge(s["kadd"], g)
                    for a in range(2):
                        dve.tensor_tensor(halves(t2[:, 1, :])[:, :, a, :], halves(kn[:, :])[:, :, 1 - a, :], S(1, a),
                                          ALU.mult).then_inc(s["knorm"], 1)

                def tile_t(g):
                    dve.wait_ge(s["tk"], g + 1)
                    sl = g % SLOTS
                    dve.tensor_copy(kT[64:128, :, 1, sl * P:(sl + 1) * P],
                                    ps[64:128, BTK, :].rearrange("p (j k) -> p j k", j=LP)).then_inc(s["kTd"], 1)

                def masked(u):
                    j, g = u % LP, u // LP
                    slots, mk = keys(u)
                    n = P * len(slots)
                    dve.wait_ge(s["sc"], u + 1)
                    if u >= 4:
                        dve.wait_ge(s["tr"], u - 3)
                    if j == 0:
                        dve.wait_ge(s["nrn"], g + 1)
                    for h in range(2):
                        dve.tensor_tensor_reduce(SP[:, u % 4, h, 0:n], ps[:, BS + u % 3, h * n:(h + 1) * n], mk,
                                                 nrn[:, g, 2 * j + h:2 * j + h + 1], BIG, ALU.add, ALU.min,
                                                 mn[:, u % 4, h:h + 1]).then_inc(s["ttr"], 1)

                def copy_p(u):
                    dve.wait_ge(s["tr"], u + 1)
                    if u >= 3:
                        dve.wait_ge(s["pv"], u - 2)
                    copy_turned(dve, u).then_inc(s["evd"], 1)

                def recip(g):
                    dve.wait_ge(s["ex"], 2 * LP * (g + 1))
                    if g >= 2:
                        dve.wait_ge(s["rb"], g - 1)
                    dve.reciprocal(rl[:, g % 2, :], ls[:, g % 2, :]).then_inc(s["rl"], 1)

                def normalise(g):
                    dve.wait_ge(s["pv"], LP * (g + 1))
                    dve.wait_ge(s["rbs"], g + 1)
                    if g >= 2:
                        dve.wait_ge(s["clo"], g - 1)
                    dve.tensor_tensor(ctxf[:, g % 2, :], ps[:, BC + g % 2, :], rbs[:, g % 2, :], ALU.mult).then_inc(s["ctx"], 1)
                    dve.wait_ge(s["ctx"], g + 1)
                    t = g % TC
                    if g >= TC and t == 0:
                        dve.wait_ge(s["w2"], KD)
                    dve.tensor_copy(ah[:, 0:LP, t * P:(t + 1) * P], ctxf[:, g % 2, :].rearrange("p (j k) -> p j k", j=LP)
                                    ).then_inc(s["chi"], 1)

                for c in range(NC):
                    split(c)
                    for t in range(TC + 1):
                        if t < TC:
                            tile_a(c * TC + t)
                        if t >= 1:
                            tile_t(c * TC + t - 1)
                    for i in range(UC + 4):
                        u = c * UC + i
                        if i < UC:
                            masked(u)
                        if 2 <= i < UC + 2 and (i - 2) % 2 == 0:
                            copy_p(u - 2)
                        if i >= 4 and (i - 4) % LP == 0:
                            recip((u - 4) // LP)
                        if i >= 7 and (i - 7) % LP == 0:
                            normalise((u - 7) // LP)
                    for k in range(KD):
                        dve.wait_ge(s["wo"], KD * c + k + 1)
                        cols = slice(1 + c * CH, 1 + (c + 1) * CH)
                        dve.tensor_tensor(xw[:, k, cols], ps[:, k, :], xw[:, k, cols], ALU.add).then_inc(s["xw"], 1)
                    dve.wait_ge(s["xw"], KD * (c + 1))
                    dve.wait_ge(s["mean"], c + 1)
                    for k, src in enumerate((xw[:, 0, 1 + c * CH:1 + (c + 1) * CH], xw[:, 1, chunk(c)])):
                        dve.tensor_tensor(hcen[:, k, :], src, ps[:, 2, :], ALU.subtract).then_inc(s["hc"], 1)
                    dve.wait_ge(s["hdev"], c + 1)
                    dve.reciprocal(hrs[:, c, :], hdev[:, c, :]).then_inc(s["rs"], 1)
                    dve.wait_ge(s["rsb"], c + 1)
                    dve.tensor_tensor(hcen[:, :, :], hcen[:, :, :], ps[:, 2:3, :].to_broadcast([P, KD, CH]),
                                      ALU.mult).then_inc(s["hn"], 1)
                    dve.wait_ge(s["hn"], c + 1)
                    if c:
                        dve.wait_ge(s["ag"], 2 * HT * c)
                    dve.tensor_copy(hh_[:, :, :], hcen[:, :, :]).then_inc(s["hhi"], 1)
                    dve.wait_ge(s["hhi"], c + 1)
                    dve.tensor_tensor(hl_[:, :, :], hcen[:, :, :], hh_[:, :, :], ALU.subtract).then_inc(s["hlo"], 1)
                    for j in range(HT):
                        n, mj = HT * c + j, rows_of(j)
                        dve.wait_ge(s["ag"], 2 * n + 2)
                        dve.wait_ge(s["ge"], n + 1)
                        if j >= 2:
                            dve.wait_ge(s["ulo"], n - 1)
                        dve.scalar_tensor_tensor(out=ctxf[0:mj, j % 2, :], in0=ps[0:mj, 4 + 2 * (j % 2), :],
                                                 scalar=b1c[0:mj, 0, j:j + 1], in1=rbs[0:mj, j % 2, :], op0=ALU.add,
                                                 op1=ALU.mult).then_inc(s["u"], 1)
                        dve.wait_ge(s["u"], n + 1)
                        dve.tensor_copy(ah[0:mj, j, :], ctxf[0:mj, j % 2, :]).then_inc(s["uhi"], 1)
                    for k in range(KD):
                        dve.wait_ge(s["w2"], KD * c + k + 1)
                        if c:
                            dve.wait_ge(s["out"], 16 * c)
                        dve.scalar_tensor_tensor(out=xout[:, k, :], in0=ps[:, k, :], scalar=b2c[:, k:k + 1],
                                                 in1=xw[:, k, 1 + c * CH:1 + (c + 1) * CH], op0=ALU.add,
                                                 op1=ALU.add).then_inc(s["xout"], 1)

            @block.gpsimd
            def _(pool):
                for c in range(NC):
                    for t in range(TC):
                        g = c * TC + t
                        pool.wait_ge(s["qrot"], 3 * (g + 1))
                        pool.tensor_tensor(t1[:, g % 2, 0, :], t1[:, g % 2, 0, :], t2[:, 0, :], ALU.add).then_inc(s["qadd"], 1)
                        pool.wait_ge(s["knorm"], 3 * (g + 1))
                        pool.tensor_tensor(t1[:, g % 2, 1, :], t1[:, g % 2, 1, :], t2[:, 1, :], ALU.add).then_inc(s["kadd"], 1)
                    for t in range(TC):
                        g = c * TC + t
                        pool.wait_ge(s["chi"], g + 1)
                        cols = slice(t * P, (t + 1) * P)
                        pool.tensor_tensor(al[:, 0:LP, cols], ctxf[:, g % 2, :].rearrange("p (j k) -> p j k", j=LP),
                                           ah[:, 0:LP, cols], ALU.subtract).then_inc(s["clo"], 1)
                    for j in range(HT):
                        n, mj = HT * c + j, rows_of(j)
                        pool.wait_ge(s["uhi"], n + 1)
                        pool.tensor_tensor(al[0:mj, j, :], ctxf[0:mj, j % 2, :], ah[0:mj, j, :], ALU.subtract
                                           ).then_inc(s["ulo"], 1)

        with nc.Fori(0, DEPTH) as l:
            one = lambda t: t[bass.ds(l, 1)]
            with nc.Block() as block:
                @block.sync
                def _(sp):
                    with nc.allow_non_contiguous_dma(reason="bias columns"):
                        sp.dma_start(st_q, one(wqkv).rearrange("l (k p) n -> p (l k) n", p=P)).then_inc(w["load"], 16)
                        for k in range(KD):
                            sp.dma_start(st_1[k], one(w1)[:, k * P:(k + 1) * P].rearrange("l p n -> (l p) n")
                                         ).then_inc(w["load"], 16)
                        sp.dma_start(st_o, one(wo).rearrange("l (k p) n -> p (l k) n", p=P)).then_inc(w["load"], 16)
                        sp.dma_start(st_2[0:HW, 0:HT - 1, :], one(w2)[:, 0:(HT - 1) * HW].rearrange(
                            "l (k p) n -> p (l k) n", p=HW)).then_inc(w["load"], 16)
                        sp.dma_start(st_2[0:HREM, HT - 1, :], one(w2)[:, (HT - 1) * HW:HID].rearrange(
                            "l p n -> (l p) n")).then_inc(w["load"], 16)
                        sp.dma_start(st_r, rot).then_inc(w["load"], 16)
                        for i in range(2):
                            sp.dma_start(b1c[0:HW, i, 0:HT - 1], one(b1)[:, i * HID:i * HID + (HT - 1) * HW].rearrange(
                                "l (k p) -> p (l k)", p=HW)).then_inc(w["load"], 16)
                            sp.dma_start(b1c[0:HREM, i, HT - 1:HT], one(b1)[
                                :, i * HID + (HT - 1) * HW:(i + 1) * HID].rearrange("l p -> p l")).then_inc(w["load"], 16)
                        for dst, src in ((b2c, b2), (lg, ln_g), (lb, ln_b)):
                            sp.dma_start(dst[:, :], one(src).rearrange("l (k p) -> p (l k)", p=P)).then_inc(w["load"], 16)
                        for i, src in enumerate((q_scale, k_scale)):
                            sp.dma_start(qsc[:, i, :], one(src).rearrange("l d -> (l d)").partition_broadcast(P)
                                         ).then_inc(w["load"], 16)

                @block.gpsimd
                def _(pool):
                    pool.memset(mask[:, :], 0.0).then_inc(w["mask"], 1)
                    pool.wait_ge(w["mask"], 1)
                    for k, sign in enumerate((1, -1, 1)):
                        pool.affine_select(out=mask[:, k * P:(k + 1) * P], in_=mask[:, k * P:(k + 1) * P],
                                           compare_op=ALU.is_ge, fill=NEG, base=0, pattern=[[sign, P]],
                                           channel_multiplier=-sign).then_inc(w["masked"], 1)
                    pool.wait_ge(w["load"], 16 * LOADS)
                    H2 = DH // 2
                    for i in range(2):
                        for h in range(2):
                            own = qsc[:, i:i + 1, h * H2:(h + 1) * H2].to_broadcast([P, NT, H2])
                            other = qsc[:, i:i + 1, (1 - h) * H2:(2 - h) * H2].to_broadcast([P, NT, H2])
                            pool.tensor_tensor(rotC[:, i, :, h * H2:(h + 1) * H2], st_r[:, :, 3 * i, :], own,
                                               ALU.mult).then_inc(w["tab"], 1)
                            pool.tensor_tensor(rotS[:, i, :, h * H2:(h + 1) * H2], st_r[:, :, 3 * i + 1 + h, :],
                                               other, ALU.mult).then_inc(w["tab"], 1)
                    pool.wait_ge(w["tab"], 8)
                    pool.memset(xw[:, :, 0:1], 0.0).then_inc(w["zero"], 1)
                    pool.wait_ge(w["lo"], 4)
                    pool.wait_ge(w["zero"], 1)
                    for a in range(2):
                        pool.memset(kT[64 - 64 * a:128 - 64 * a, :, a, :], 0.0).then_inc(w["zero"], 1)
                        pool.wait_ge(w["zero"], 2 + a)
                    pool.wait_ge(w["masked"], 3)

                @block.tensor
                def _(pe):
                    pe.wait_ge(w["load"], 16 * LOADS)
                    for i in range(2):
                        for j in range(HT):
                            f0, m = i * HID + j * HW, rows_of(j)
                            for k in range(KD):
                                last = pe.matmul(ps[0:m, 0, i * HT + j:i * HT + j + 1], st_1[k][:, f0:f0 + m],
                                                 lb[:, k:k + 1], start=(k == 0), stop=(k == KD - 1))
                    last.then_inc(w["bias"], 1)

                @block.vector
                def _(dve):
                    dve.wait_ge(w["load"], 16 * LOADS)
                    dve.wait_ge(w["bias"], 1)
                    bias = ps[:, 0, 0:2 * HT].rearrange("p (i j) -> p i j", i=2)
                    dve.tensor_tensor(b1c[0:HW, :, 0:HT - 1], b1c[0:HW, :, 0:HT - 1], bias[0:HW, :, 0:HT - 1], ALU.add
                                      ).then_inc(w["biased"], 1)
                    dve.tensor_tensor(b1c[0:HREM, :, HT - 1], b1c[0:HREM, :, HT - 1], bias[0:HREM, :, HT - 1],
                                      ALU.add).then_inc(w["biased"], 1)
                    for k in range(KD):
                        dve.tensor_scalar(st_1[k], st_1[k], lg[:, k:k + 1], None, ALU.mult).then_inc(w["scaled"], 1)
                    n_hi = 0
                    parts = [(Wq_hi[:, :, :], Wq_lo[:, :, :], st_q)]
                    parts += [(W1_hi[:, k, :], W1_lo[:, k, :], st_1[k]) for k in range(KD)]
                    parts += [(Wo_hi[:, :, :], Wo_lo[:, :, :], st_o)]
                    parts += [(W2_hi[0:HW, 0:HT - 1, :], W2_lo[0:HW, 0:HT - 1, :], st_2[0:HW, 0:HT - 1, :])]
                    parts += [(W2_hi[0:HREM, HT - 1, :], W2_lo[0:HREM, HT - 1, :], st_2[0:HREM, HT - 1, :])]
                    dve.wait_ge(w["scaled"], KD)
                    for hi, lo, src in parts:
                        dve.tensor_copy(hi, src).then_inc(w["hi"], 1)
                        n_hi += 1
                        dve.wait_ge(w["hi"], n_hi)
                        dve.tensor_tensor(lo, src, hi, ALU.subtract).then_inc(w["lo"], 1)
                    dve.wait_ge(w["lo"], len(parts))
                    dve.wait_ge(w["biased"], 2)
            clear(nc, w)

            with nc.Fori(0, B) as b:
                with nc.Block() as block:
                    layer_block(block, b)
                clear(nc, s)


def stage_g(nc, x, A, state, out, ident, eps, ps):
    Wq, Wkv_down, Wk_up, Wv_up, Wout = A
    with ExitStack() as ctx:
        sb = lambda n, sh, dt=F32: ctx.enter_context(nc.sbuf_tensor(n, sh, dt))
        two = lambda n, sh: (sb(n + "_hi", sh, F32R), sb(n + "_lo", sh, F32R))
        Gh, Gl = two("g_wq", [P, KD, GH * DH])
        Oh, Ol = two("g_wo", [P, GP, D])
        Kh, Kl = two("g_wk", [P, KD, 2 * DH])
        mask = sb("g_mask", [P, N])
        xtok = sb("g_xtok", [P, NT, D])
        xn = sb("g_xn", [P, NT, D])
        xnh, xnl = two("g_xn2", [P, KD, N])
        fT = sb("g_fT", [P, KD, N])
        lath, latl = two("g_lat", [P, N])
        latf = sb("g_latf", [DH, N])
        latV = sb("g_latV", [P, NT, DH])
        qst = sb("g_q", [P, GH, CH], F32R)
        SP = sb("g_sp", [P, 2, 4, N])
        PT = sb("g_pt", [P, 4, CH])
        rbs = sb("g_rbs", [P, 2, 2 * P])
        ctxf = sb("g_ctxf", [P, 2, 2 * P])
        ch, cl = two("g_ctx", [P, GP, CH])
        prod = sb("g_prod", [P, KD, CH])
        bst = sb("g_bst", [P, NT, 6])
        mv = sb("g_mv", [P, NT, 2])
        dev = sb("g_dev", [P, NT])
        rstd = sb("g_rstd", [P, NT])
        mn = sb("g_mn", [P, 2, 4])
        ls = sb("g_ls", [P, 2, 4])
        rl = sb("g_rl", [P, 2, 4])

        w = semaphores(nc, ctx, "gw_", "load mask tq tk g o hi lo copied khi klo ghi glo")
        s = semaphores(nc, ctx, "g_", "x_in stats moments dev rstd xn xnT xhi xlo f_in silu lat lathi latf latlo "
                 "vt v q qhi qlo sc ttr ex tr eva evd pv rl rb rbs ctx chi clo wo prod back y out")

        sflat = SP[:, :, :, :].rearrange("p a b c -> p (a b c)")
        xflat = xtok[:, :, :].rearrange("p a b -> p (a b)")
        HD_ = GH * DH
        wq_s = sflat[:, 0:KD * HD_].rearrange("p (k n) -> p k n", k=KD)
        wk_s = sflat[0:DH, 2048:2048 + HD_]
        wv_s = sflat[0:DH, 3072:3072 + HD_]
        wo_s = sflat[:, 4096:4096 + GP * D].rearrange("p (j n) -> p j n", j=GP)
        wqT = sflat[:, 6144:6144 + GP * D].rearrange("p (j n) -> p j n", j=GP)
        wkT = xflat[:, 0:GP * DH].rearrange("p (j n) -> p j n", j=GP)
        wvT = xflat[:, 512:512 + GP * DH].rearrange("p (j n) -> p j n", j=GP)
        kd_s = xflat[:, 1024:1024 + KD * DH].rearrange("p (k n) -> p k n", k=KD)

        with nc.Block() as block:
            @block.sync
            def _(sp):
                for dst, src in ((wq_s, Wq.rearrange("(k p) h d -> p k (h d)", p=P)),
                                 (wk_s, Wk_up.rearrange("c h d -> c (h d)")),
                                 (wv_s, Wv_up.rearrange("c h d -> c (h d)")),
                                 (wo_s, Wout.rearrange("h d o -> (h d) o").rearrange("(j p) o -> p j o", p=P)),
                                 (kd_s, Wkv_down.rearrange("(k p) c -> p k c", p=P))):
                    sp.dma_start(dst, src).then_inc(w["load"], 16)

            @block.gpsimd
            def _(pool):
                pool.memset(mask[:, :], 0.0).then_inc(w["mask"], 1)
                pool.wait_ge(w["mask"], 1)
                pool.affine_select(out=mask[:, N - P:N], in_=mask[:, N - P:N], compare_op=ALU.is_ge, fill=NEG,
                                   base=0, pattern=[[-1, P]], channel_multiplier=1).then_inc(w["mask"], 1)
                pool.wait_ge(w["mask"], 2)

            @block.tensor
            def _(pe):
                pe.wait_ge(w["load"], 16 * 5)
                for j in range(GP):
                    for k in range(KD):
                        last = pe.transpose(ps[:, j // 2, (j % 2) * D + k * P:(j % 2) * D + (k + 1) * P],
                                            wq_s[:, k, j * P:(j + 1) * P], ident[:, :])
                last.then_inc(w["tq"], 1)
                for bank, src in ((4, wk_s), (5, wv_s)):
                    for j in range(GP):
                        last = pe.transpose(ps[:, bank, j * DH:(j + 1) * DH], src[:, j * P:(j + 1) * P],
                                            ident[0:DH, 0:DH])
                    last.then_inc(w["tk"], 1)
                pe.wait_ge(w["copied"], 6)
                for k in range(KD):
                    for a in range(2):
                        for j in range(GP):
                            last = pe.matmul(ps[:, 2 * k + a, j * DH:(j + 1) * DH],
                                             wqT[64 * a:64 * a + 64, j, k * P:(k + 1) * P],
                                             wkT[64 * a:64 * a + 64, j, :], start=True, stop=True)
                        last.then_inc(w["g"], 1)
                pe.wait_ge(w["glo"], 4)
                for a in range(2):
                    for j in range(GP):
                        last = pe.matmul(ps[64 * a:64 * a + 64, 4 * a + j // 2, (j % 2) * D:(j % 2 + 1) * D],
                                         wvT[64 * a:64 * a + 64, j, :], wo_s[64 * a:64 * a + 64, j, :],
                                         start=True, stop=True)
                    last.then_inc(w["o"], 1)

            @block.vector
            def _(dve):
                dve.wait_ge(w["load"], 16 * 5)
                for i in range(2):
                    dve.tensor_copy(Kh[:, :, i * DH:(i + 1) * DH], kd_s).then_inc(w["khi"], 1)
                dve.wait_ge(w["khi"], 2)
                for i in range(2):
                    dve.tensor_tensor(Kl[:, :, i * DH:(i + 1) * DH], kd_s, Kh[:, :, i * DH:(i + 1) * DH],
                                      ALU.subtract).then_inc(w["klo"], 1)
                dve.wait_ge(w["tq"], 1)
                for i in range(4):
                    dve.tensor_copy(wqT[:, 2 * i:2 * i + 2, :], ps[:, i, :].rearrange("p (j n) -> p j n", j=2)
                                    ).then_inc(w["copied"], 1)
                for i, dst in enumerate((wkT, wvT)):
                    dve.wait_ge(w["tk"], i + 1)
                    dve.tensor_copy(dst, ps[:, 4 + i, :].rearrange("p (j n) -> p j n", j=GP)).then_inc(w["copied"], 1)
                for k in range(KD):
                    for a in range(2):
                        i = 2 * k + a
                        dve.wait_ge(w["g"], i + 1)
                        view = lambda t: t[:, k, :].rearrange("p (j a n) -> p j a n", j=GP, a=2)[:, :, a, :]
                        src = ps[:, i, :].rearrange("p (j n) -> p j n", j=GP)
                        dve.tensor_scalar(view(Gh), src, DH ** -0.5, None, ALU.mult).then_inc(w["ghi"], 1)
                        dve.wait_ge(w["ghi"], i + 1)
                        dve.scalar_tensor_tensor(out=view(Gl), in0=src, scalar=DH ** -0.5, in1=view(Gh),
                                                 op0=ALU.mult, op1=ALU.subtract).then_inc(w["glo"], 1)
                for a in range(2):
                    dve.wait_ge(w["o"], a + 1)
                    rows = slice(64 * a, 64 * a + 64)
                    for i in range(4):
                        src = ps[rows, 4 * a + i, :].rearrange("p (j n) -> p j n", j=2)
                        dve.tensor_copy(Oh[rows, 2 * i:2 * i + 2, :], src).then_inc(w["hi"], 1)
                        dve.wait_ge(w["hi"], 4 * a + i + 1)
                        dve.tensor_tensor(Ol[rows, 2 * i:2 * i + 2, :], src, Oh[rows, 2 * i:2 * i + 2, :],
                                          ALU.subtract).then_inc(w["lo"], 1)
                dve.wait_ge(w["lo"], 8)
                dve.wait_ge(w["klo"], 2)
        clear(nc, w)

        UQ = GH // 4
        UC = TC * UQ
        tiles_of = lambda u: u // UQ + 1
        first = [sum(tiles_of(v) for v in range(u)) for u in range(NC * UC + 1)]
        BT, BC = 4, 6
        place = lambda h: (h % 2) * 2 + h // 2
        evs = lambda n, par: (n - par + 1) // 2 if n > par else 0
        chunk = lambda c: slice(c * CH, (c + 1) * CH)

        with nc.Fori(0, B) as b:
            with nc.Block() as block:
                @block.sync
                def _(sp):
                    sp.dma_start(xtok[:, :, :], x[bass.ds(b, 1)].rearrange("b (t p) d -> p (b t) d", p=P)
                                 ).then_inc(s["x_in"], 16)
                    sp.dma_start(fT[:, :, :], state[bass.ds(b, 1)].rearrange("b p k n -> p (b k) n")
                                 ).then_inc(s["f_in"], 16)
                    for c in range(NC):
                        sp.wait_ge(s["y"], 2 * (c + 1))
                        sp.dma_start(out[bass.ds(b, 1), chunk(c)].rearrange("b (t p) d -> p (b t) d", p=P),
                                     xtok[:, c * TC:(c + 1) * TC, :]).then_inc(s["out"], 16)
                    sp.wait_ge(s["out"], 16 * NC)

                @block.tensor
                def _(pe):
                    transpose_tokens(pe, s, xn, ps, ident)
                    pe.wait_ge(s["xlo"], KD * NC)
                    for c in range(NC):
                        three(pe, ps[:, 4 + c, :], [(Kh[:, k, :], Kl[:, k, :], xnh[:, k, chunk(c)],
                                                     xnl[:, k, chunk(c)]) for k in range(KD)]).then_inc(s["lat"], 1)
                    pe.wait_ge(s["latf"], NC)
                    for t in range(NT):
                        last = pe.transpose(ps[:, 6, t * DH:(t + 1) * DH], latf[:, t * P:(t + 1) * P],
                                            ident[0:DH, 0:DH])
                    last.then_inc(s["vt"], 1)

                    def queries(c, j):
                        n = c * GP + j
                        if j >= 4:
                            pe.wait_ge(s["qlo"], 2 * (n - 3))
                        elif c:
                            pe.wait_ge(s["prod"], KD * c)
                        three(pe, ps[:, j % 4, :], [(Gh[:, k, j * P:(j + 1) * P], Gl[:, k, j * P:(j + 1) * P],
                                                     xnh[:, k, chunk(c)], xnl[:, k, chunk(c)])
                                                    for k in range(KD)]).then_inc(s["q"], 1)

                    def scores(u, h):
                        t, n = u // UQ, P * tiles_of(u)
                        i = 4 * u + h
                        if u % UC == 0 and h == 0:
                            pe.wait_ge(s["qlo"], GH * (u // UC + 1))
                            pe.wait_ge(s["latlo"], NC)
                        if i % (4 * UC) >= 2:
                            pe.wait_ge(s["ttr"], i - 1)
                        head, tok = 4 * (u % UQ) + h, slice(t % TC * P, (t % TC + 1) * P)
                        for k in range(-(-n // CH)):
                            cols = slice(k * CH, min(n, (k + 1) * CH))
                            o = ps[:, 2 * (i % 2) + k, 0:cols.stop - cols.start]
                            pe.matmul(o, qst[:, head, tok], lath[:, cols], start=True, stop=False)
                            last = pe.matmul(o, qst[:, head, tok], latl[:, cols], start=False, stop=True)
                        last.then_inc(s["sc"], 1)

                    def turn(u, k):
                        n = first[u] + k
                        if k == 0:
                            pe.wait_ge(s["ex"], 4 * (u + 1))
                            if u == 0:
                                pe.wait_ge(s["v"], 1)
                        if n >= 2:
                            pe.wait_ge(s["eva"] if n % 2 else s["evd"], n // 2)
                        if k == 0 and u and u % UC == 0:
                            pe.wait_ge(s["y"], 2 * (u // UC))
                        for h in range(4):
                            c0 = place(h) * P
                            last = pe.transpose(ps[:, BT + n % 2, c0:c0 + P], SP[:, u % 2, h, k * P:(k + 1) * P],
                                                ident[:, :])
                        last.then_inc(s["tr"], 1)

                    def weigh(u, k):
                        n = first[u] + k
                        pe.wait_ge(s["eva"] if n % 2 else s["evd"], n // 2 + 1)
                        if k == 0 and u >= 2:
                            pe.wait_ge(s["ctx"], u - 1)
                        for a in range(2):
                            last = pe.matmul(ps[64 * a:64 * a + 64, BC + u % 2, 0:2 * P], latV[:, k, :],
                                             PT[:, n % 4, a * 2 * P:(a + 1) * 2 * P], start=(k == 0),
                                             stop=(k == tiles_of(u) - 1), skip_group_check=True)
                        last.then_inc(s["pv"], 1)

                    def spread(u):
                        pe.wait_ge(s["rl"], u + 1)
                        for j in range(2):
                            for h in range(2):
                                last = pe.matmul(ps[64 * h:64 * h + 64, BC + u % 2, (2 + j) * P:(3 + j) * P],
                                                 rl[:, u % 2, 2 * j + h:2 * j + h + 1].to_broadcast([P, DH]),
                                                 ident[:, :], start=True, stop=True, skip_group_check=True)
                        last.then_inc(s["rb"], 1)

                    for c in range(NC):
                        for j in range(GP):
                            queries(c, j)
                        for u in range(c * UC, (c + 1) * UC + 2):
                            new, old = u < (c + 1) * UC, c * UC < u <= (c + 1) * UC
                            nk = tiles_of(u - 1) if old else 0
                            for i in range(max(4, nk + 1)):
                                if new and i < 4:
                                    scores(u, i)
                                if i < nk:
                                    turn(u - 1, i)
                                if i == 1 and u >= c * UC + 2:
                                    spread(u - 2)
                                if 1 <= i <= nk:
                                    weigh(u - 1, i - 1)
                        pe.wait_ge(s["clo"], UC * (c + 1))
                        for m in range(KD):
                            f = slice(m * P, (m + 1) * P)
                            three(pe, ps[:, m, :], [(Oh[:, j, f], Ol[:, j, f], ch[:, j, :], cl[:, j, :])
                                                    for j in range(GP)]).then_inc(s["wo"], 1)
                        pe.wait_ge(s["prod"], KD * (c + 1))
                        for t in range(TC):
                            for m in range(KD):
                                last = pe.transpose(ps[:, BT + t // 2, (t % 2) * D + m * P:(t % 2) * D + (m + 1) * P],
                                                    prod[:, m, t * P:(t + 1) * P], ident[:, :])
                            if t % 2:
                                last.then_inc(s["back"], 1)

                @block.scalar
                def _(act):
                    deviations(act, s, mv, dev, eps)
                    act.wait_ge(s["f_in"], 16)
                    act.activation(fT[:, :, :], fT[:, :, :], ACT.Silu).then_inc(s["silu"], 1)
                    for i in range(KD * NC):
                        act.wait_ge(s["xnT"], i + 1)
                        act.activation(xnh[:, i // NC, chunk(i % NC)], ps[:, i, :], ACT.Copy).then_inc(s["xhi"], 1)
                    for c in range(NC):
                        act.wait_ge(s["lat"], c + 1)
                        act.activation(lath[:, chunk(c)], ps[:, 4 + c, :], ACT.Copy).then_inc(s["lathi"], 1)
                        act.activation(latf[:, chunk(c)], ps[0:DH, 4 + c, :], ACT.Copy).then_inc(s["latf"], 1)
                    act.wait_ge(s["vt"], 1)
                    act.activation(latV[:, :, :], ps[:, 6, :].rearrange("p (t n) -> p t n", t=NT), ACT.Copy
                                   ).then_inc(s["v"], 1)

                    def exps(u, h):
                        n = P * tiles_of(u)
                        act.wait_ge(s["ttr"], 4 * u + h + 1)
                        if h == 0 and u >= 2:
                            act.wait_ge(s["rl"], u - 1)
                        act.activation(SP[:, u % 2, h, 0:n], SP[:, u % 2, h, 0:n], ACT.Exp, bias=mn[:, u % 2, h:h + 1],
                                       scale=-1.0, accum_out=ls[:, u % 2, h:h + 1]).then_inc(s["ex"], 1)

                    def copy(u, k):
                        n = first[u] + k
                        if n % 2:
                            act.wait_ge(s["tr"], n + 1)
                            if n >= 4:
                                act.wait_ge(s["pv"], n - 3)
                            act.activation(PT[:, n % 4, :], ps[:, BT + n % 2, :], ACT.Copy).then_inc(s["eva"], 1)

                    def copy_r(u):
                        act.wait_ge(s["rb"], u + 1)
                        if u >= 2:
                            act.wait_ge(s["ctx"], u - 1)
                        act.activation(rbs[:, u % 2, :], ps[:, BC + u % 2, 2 * P:4 * P], ACT.Copy).then_inc(s["rbs"], 1)

                    for c in range(NC):
                        for j in range(GP):
                            n = c * GP + j
                            act.wait_ge(s["q"], n + 1)
                            if c and j == 0:
                                act.wait_ge(s["sc"], 4 * UC * c)
                            for a in range(2):
                                rows = slice(64 * a, 64 * a + 64)
                                act.activation(qst[rows, 2 * j + a, :], ps[rows, j % 4, :], ACT.Copy).then_inc(s["qhi"], 1)
                        for u in range(c * UC, (c + 1) * UC + 2):
                            new, old = u < (c + 1) * UC, c * UC < u <= (c + 1) * UC
                            nk = tiles_of(u - 1) if old else 0
                            for i in range(max(4, nk + 1)):
                                if new and i < 4:
                                    exps(u, i)
                                if i < nk:
                                    copy(u - 1, i)
                                if i == 1 and u >= c * UC + 2:
                                    copy_r(u - 2)

                @block.vector
                def _(dve):
                    layernorm_tokens(dve, s, xtok, xn, bst, mv, dev, rstd)
                    for i in range(KD * NC):
                        dve.wait_ge(s["xhi"], i + 1)
                        dve.tensor_tensor(xnl[:, i // NC, chunk(i % NC)], ps[:, i, :], xnh[:, i // NC, chunk(i % NC)],
                                          ALU.subtract).then_inc(s["xlo"], 1)
                    for c in range(NC):
                        dve.wait_ge(s["latf"], c + 1)
                        dve.tensor_tensor(latl[:, chunk(c)], ps[:, 4 + c, :], lath[:, chunk(c)], ALU.subtract
                                          ).then_inc(s["latlo"], 1)

                    def masked(u, h):
                        n, i = P * tiles_of(u), 4 * u + h
                        dve.wait_ge(s["sc"], i + 1)
                        if h == 0 and u >= 2:
                            dve.wait_ge(s["tr"], first[u - 1])
                        src = ps[:, 2 * (i % 2):2 * (i % 2) + 2, :].rearrange("p a b -> p (a b)")[:, 0:n]
                        dve.tensor_tensor_reduce(SP[:, u % 2, h, 0:n], src, mask[:, N - n:N], -1.0, BIG, ALU.add,
                                                 ALU.min, mn[:, u % 2, h:h + 1]).then_inc(s["ttr"], 1)

                    def copy(u, k):
                        n = first[u] + k
                        if n % 2 == 0:
                            dve.wait_ge(s["tr"], n + 1)
                            if n >= 4:
                                dve.wait_ge(s["pv"], n - 3)
                            dve.tensor_copy(PT[:, n % 4, :], ps[:, BT + n % 2, :]).then_inc(s["evd"], 1)

                    def recip(u):
                        dve.wait_ge(s["ex"], 4 * (u + 1))
                        if u >= 2:
                            dve.wait_ge(s["rb"], u - 1)
                        dve.reciprocal(rl[:, u % 2, :], ls[:, u % 2, :]).then_inc(s["rl"], 1)

                    def normalise(u):
                        dve.wait_ge(s["pv"], first[u + 1])
                        dve.wait_ge(s["rbs"], u + 1)
                        if u >= 2:
                            dve.wait_ge(s["clo"], u - 1)
                        if u and u % UC == 0:
                            dve.wait_ge(s["wo"], KD * (u // UC))
                        dve.tensor_tensor(ctxf[:, u % 2, :], ps[:, BC + u % 2, 0:2 * P], rbs[:, u % 2, :], ALU.mult
                                          ).then_inc(s["ctx"], 1)
                        dve.wait_ge(s["ctx"], u + 1)
                        j, t = 2 * (u % UQ), u // UQ % TC
                        dve.tensor_copy(ch[:, j:j + 2, t * P:(t + 1) * P],
                                        ctxf[:, u % 2, :].rearrange("p (j k) -> p j k", j=2)).then_inc(s["chi"], 1)

                    for c in range(NC):
                        for j in range(GP):
                            n = c * GP + j
                            for a in range(2):
                                here, there = slice(64 * a, 64 * a + 64), slice(64 - 64 * a, 128 - 64 * a)
                                dve.wait_ge(s["qhi"], 2 * n + 2)
                                dve.tensor_tensor(qst[there, 2 * j + a, :], ps[here, j % 4, :], qst[here, 2 * j + a, :],
                                                  ALU.subtract).then_inc(s["qlo"], 1)
                        for u in range(c * UC, (c + 1) * UC + 2):
                            new, old = u < (c + 1) * UC, c * UC < u <= (c + 1) * UC
                            nk = tiles_of(u - 1) if old else 0
                            for i in range(max(4, nk + 1)):
                                if new and i < 4:
                                    masked(u, i)
                                if i == 0 and old:
                                    recip(u - 1)
                                if i < nk:
                                    copy(u - 1, i)
                                if i == 2 and u >= c * UC + 2:
                                    normalise(u - 2)
                        dve.wait_ge(s["silu"], 1)
                        for m in range(KD):
                            dve.wait_ge(s["wo"], KD * c + m + 1)
                            dve.tensor_tensor(prod[:, m, :], ps[:, m, :], fT[:, m, chunk(c)], ALU.mult
                                              ).then_inc(s["prod"], 1)
                        for i in range(2):
                            dve.wait_ge(s["back"], 2 * c + i + 1)
                            rows = xtok[:, c * TC + 2 * i:c * TC + 2 * i + 2, :]
                            dve.tensor_tensor(rows, ps[:, BT + i, :].rearrange("p (t d) -> p t d", t=2), rows, ALU.add
                                              ).then_inc(s["y"], 1)

                @block.gpsimd
                def _(pool):
                    for u in range(NC * UC):
                        pool.wait_ge(s["chi"], u + 1)
                        j, t = 2 * (u % UQ), u // UQ % TC
                        cols = slice(t * P, (t + 1) * P)
                        pool.tensor_tensor(cl[:, j:j + 2, cols], ctxf[:, u % 2, :].rearrange("p (j k) -> p j k", j=2),
                                           ch[:, j:j + 2, cols], ALU.subtract).then_inc(s["clo"], 1)
            clear(nc, s)


def build(nc, x, Wq, Wkv_down, Wk_up, Wv_up, Wout, wqkv, q_scale, k_scale, wo, ln_g, ln_b, w1, b1, w2, b2,
          rot, out):
    state = nc.dram_tensor("state", [B, P, KD, N], F32).ap()
    with ExitStack() as ctx:
        ident = ctx.enter_context(nc.sbuf_tensor("ident", [P, P], F32))
        ones = ctx.enter_context(nc.sbuf_tensor("ones", [P, P], F32))
        eps = ctx.enter_context(nc.sbuf_tensor("eps", [P, 1], F32))
        ps = ctx.enter_context(nc.psum_tensor("ps", [P, 8, CH], F32))
        setup(nc, ident, ones, eps, semaphores(nc, ctx, "s_", "const"))
        stage_n(nc, x, state, ident, eps, ps)
        stage_l(nc, (wqkv, q_scale, k_scale, wo, ln_g, ln_b, w1, b1, w2, b2, rot), state, ident, ones, eps, ps)
        stage_g(nc, x, (Wq, Wkv_down, Wk_up, Wv_up, Wout), state, out, ident, eps, ps)


_INS = ["L0_attn_x_bld", "L0_attn_Wq", "L0_attn_Wkv_down", "L0_attn_Wk_up", "L0_attn_Wv_up", "L0_attn_Wout",
        "L0_ffn_wqkv", "L0_ffn_q_scale", "L0_ffn_k_scale", "L0_ffn_wo", "L0_ffn_ln_g", "L0_ffn_ln_b",
        "L0_ffn_w1", "L0_ffn_b1", "L0_ffn_w2", "L0_ffn_b2"]


def kernel(**inputs):
    import numpy as _np
    import concourse.bacc as _bacc
    from concourse import mybir as _mybir
    from concourse.bass_utils import run_bass_kernel_spmd as _run

    nc = _bacc.Bacc("TRN2", target_bir_lowering=False, num_devices=1)
    arrays, args = {}, []
    for name in _INS:
        a = _np.ascontiguousarray(inputs[name])
        arrays[f"in_{name}_dram"] = a
        args.append(nc.dram_tensor(f"in_{name}_dram", a.shape, _mybir.dt.from_np(a.dtype), kind="ExternalInput").ap())
    rot = rotary_tables()
    arrays["rotary_dram"] = rot
    args.append(nc.dram_tensor("rotary_dram", rot.shape, _mybir.dt.from_np(rot.dtype), kind="ExternalInput").ap())
    args.append(nc.dram_tensor("out_0_dram", (B, N, D), _mybir.dt.float32, kind="ExternalOutput").ap())
    build(nc, *args)
    r = _run(nc, [arrays], core_ids=[0])
    return r.results[0]["out_0_dram"]
```

```python
from contextlib import ExitStack

import numpy as np

import concourse.bass as bass
from concourse import mybir

F32 = mybir.dt.float32
F32R = mybir.dt.float32r
ALU = mybir.AluOpType
ACT = mybir.ActivationFunctionType
AX_X = mybir.AxisListType.X

P = 128
B, N, D = 4, 1024, 256
KD = D // P
NT = N // P
CH = 512
NC = N // CH
SB = 4
QN = SB * NC
TC = CH // P
DH = 64
LH = 8
LP = LH // 2
INNER = LH * DH
DEPTH = 2
HID = 682
HT = -(-HID // P)
HW = -(-HID // HT)
HREM = HID - (HT - 1) * HW
GH = 16
GP = GH // 2
EPS = 1e-5
NEG = -1e30
BIG = 3e38
SLOTS = 5


def rows_of(j):
    return HW if j < HT - 1 else HREM


def rotary_tables():
    f = np.float32
    half = np.arange(0, DH, 2, dtype=f)
    inv = (f(1.0) / np.power(f(10000.0), half / f(DH))).astype(f)
    t = np.arange(N, dtype=f)
    freqs = (t[:, None] * inv[None, :]).astype(f)
    base = ((half + f(0.4 * DH)) / f(1.4 * DH)).astype(f)
    power = ((t - f(N // 2)) / f(64.0)).astype(f)
    scale = np.power(base[None, :], power[:, None]).astype(f)
    cos, sin = np.cos(freqs).astype(f), np.sin(freqs).astype(f)
    six = np.stack([cos * scale, -sin * scale, sin * scale, cos / scale, -sin / scale, sin / scale], 1)
    return np.ascontiguousarray(six.reshape(NT, P, 6, DH // 2).transpose(1, 0, 2, 3).astype(f))


def semaphores(nc, ctx, prefix, names):
    return {n: ctx.enter_context(nc.semaphore(prefix + n)) for n in names.split()}


def clear(nc, sems):
    with nc.Block() as block:
        @block.gpsimd
        def _(pool):
            for sem in sems.values():
                pool.sem_clear(sem)


def three(pe, out, pairs, start=True, stop=True):
    last, n = None, len(pairs)
    for i, (wh, wl, xh, xl) in enumerate(pairs):
        pe.matmul(out, wh, xh, start=start and i == 0, stop=False)
        pe.matmul(out, wh, xl, start=False, stop=False)
        last = pe.matmul(out, wl, xh, start=False, stop=stop and i == n - 1)
    return last


def setup(nc, ident, ones, eps, s):
    with nc.Block() as block:
        @block.gpsimd
        def _(pool):
            pool.memset(ident[:, :], 0.0).then_inc(s["const"], 1)
            pool.memset(ones[:, :], 1.0 / D).then_inc(s["const"], 1)
            pool.memset(eps[:, :], EPS).then_inc(s["const"], 1)
            pool.wait_ge(s["const"], 3)
            pool.affine_select(out=ident[:, :], in_=ident[:, :], compare_op=ALU.not_equal, fill=1.0,
                               base=0, pattern=[[-1, P]], channel_multiplier=1).then_inc(s["const"], 1)
            pool.wait_ge(s["const"], 4)
    clear(nc, s)


def layernorm_tokens(dve, s, xtok, xn, bst, mv, dev, rstd):
    dve.wait_ge(s["x_in"], 16)
    for t in range(NT):
        dve.bn_stats(bst[:, t, :], xtok[:, t, :]).then_inc(s["stats"], 1)
    for t in range(NT):
        dve.wait_ge(s["stats"], t + 1)
        dve.bn_aggr(mv[:, t, :], bst[:, t, :]).then_inc(s["moments"], 1)
    dve.wait_ge(s["dev"], 1)
    dve.reciprocal(rstd[:, :], dev[:, :]).then_inc(s["rstd"], 1)
    dve.wait_ge(s["rstd"], 1)
    for t in range(NT):
        dve.tensor_scalar(xn[:, t, :], xtok[:, t, :], mv[:, t, 0:1], rstd[:, t:t + 1],
                          ALU.subtract, ALU.mult).then_inc(s["xn"], 1)


def deviations(act, s, mv, dev, eps):
    act.wait_ge(s["moments"], NT)
    act.activation(dev[:, :], mv[:, :, 1], ACT.Sqrt, bias=eps[:, :]).then_inc(s["dev"], 1)


def transpose_tokens(pe, s, xn, ps, ident):
    for kt in range(KD):
        for c in range(NC):
            for t in range(TC):
                g = c * TC + t
                pe.wait_ge(s["xn"], g + 1)
                last = pe.transpose(ps[:, kt * NC + c, t * P:(t + 1) * P], xn[:, g, kt * P:(kt + 1) * P],
                                    ident[:, :])
            last.then_inc(s["xnT"], 1)


def stage_n(nc, x, xnorm, state, ident, eps, ps):
    with ExitStack() as ctx:
        sb = lambda n, sh, dt=F32: ctx.enter_context(nc.sbuf_tensor(n, sh, dt))
        s = semaphores(nc, ctx, "n_", "x_in stats moments dev rstd xn xnT copied out")
        xtok = sb("n_xtok", [P, NT, D])
        xn = sb("n_xn", [P, NT, D])
        xT = sb("n_xT", [P, KD, N])
        bst = sb("n_bst", [P, NT, 6])
        mv = sb("n_mv", [P, NT, 2])
        dev = sb("n_dev", [P, NT])
        rstd = sb("n_rstd", [P, NT])
        with nc.Fori(0, B) as b:
            with nc.Block() as block:
                @block.sync
                def _(sp):
                    sp.dma_start(xtok[:, :, :], x[bass.ds(b, 1)].rearrange("b (t p) d -> p (b t) d", p=P)
                                 ).then_inc(s["x_in"], 16)
                    sp.wait_ge(s["copied"], KD * NC)
                    for dst in (xnorm, state):
                        sp.dma_start(dst[bass.ds(b, 1)].rearrange("b p k n -> p (b k) n"), xT[:, :, :]
                                     ).then_inc(s["out"], 16)
                    sp.wait_ge(s["out"], 16 * 2)

                @block.vector
                def _(dve):
                    layernorm_tokens(dve, s, xtok, xn, bst, mv, dev, rstd)

                @block.tensor
                def _(pe):
                    transpose_tokens(pe, s, xn, ps, ident)

                @block.scalar
                def _(act):
                    deviations(act, s, mv, dev, eps)
                    for i in range(KD * NC):
                        act.wait_ge(s["xnT"], i + 1)
                        act.activation(xT[:, i // NC, (i % NC) * CH:(i % NC + 1) * CH], ps[:, i, :],
                                       ACT.Copy).then_inc(s["copied"], 1)
            clear(nc, s)


def stage_l(nc, A, state, ident, ones, eps, ps):
    (wqkv, q_scale, k_scale, wo, ln_g, ln_b, w1, b1, w2, b2, rot) = A
    with ExitStack() as ctx:
        sb = lambda n, sh, dt=F32: ctx.enter_context(nc.sbuf_tensor(n, sh, dt))
        two = lambda n, sh: (sb(n + "_hi", sh, F32R), sb(n + "_lo", sh, F32R))
        Wq_hi, Wq_lo = two("l_wqkv", [P, KD, 3 * INNER])
        W1_hi, W1_lo = two("l_w1", [P, KD, 2 * HID])
        W2_hi, W2_lo = two("l_w2", [P, HT, D])
        Wo_hi, Wo_lo = two("l_wo", [P, LP, D])
        b1c = sb("l_b1", [P, 2, HT])
        b2c = sb("l_b2", [P, KD])
        lg = sb("l_lg", [P, KD])
        lb = sb("l_lb", [P, KD])
        qsc = sb("l_qsc", [P, 2, DH])
        rotC = sb("l_rotC", [P, 2, NT, DH])
        rotS = sb("l_rotS", [P, 2, NT, DH])
        mask = sb("l_mask", [P, 3 * P])
        xw = sb("l_xw", [P, NC, KD, CH + 1])
        xout = sb("l_xout", [P, KD, CH])
        xh, xl = two("l_x", [P, KD, CH])
        hh_, hl_ = two("l_h", [P, KD, CH])
        ah, al = two("l_act", [P, HT, CH])
        qT = sb("l_qT", [P, LP, CH])
        kT = sb("l_kT", [P, LP, 2, SLOTS * P])
        vv = sb("l_v", [P, SLOTS, INNER])
        sq = sb("l_sq", [P, 2 * CH])
        t1 = sb("l_t1", [P, 2, 2, INNER])
        t2 = sb("l_t2", [P, 2, INNER])
        kn = sb("l_kn", [P, INNER])
        ssq = sb("l_ssq", [P, 2, 2 * LH])
        norm = sb("l_norm", [P, 2, 2 * LH])
        rn = sb("l_rn", [P, 2, 2 * LH])
        hdev = sb("l_hdev", [P, 2, TC])
        hrs = sb("l_hrs", [P, 2, TC])
        nrn = sb("l_nrn", [P, NT, LH])
        SP = sb("l_sp", [P, 4, 2, 2 * P])
        mn = sb("l_mn", [P, 4, 2])
        ls = sb("l_ls", [P, 2, LH])
        rl = sb("l_rl", [P, 2, LH])
        PT = sb("l_pt", [P, 3, CH])
        rbs = sb("l_rbs", [P, 2, CH])
        ctxf = sb("l_ctxf", [P, 2, CH])
        assert LP * P == CH

        w = semaphores(nc, ctx, "lw_", "load mask masked tab bias biased scaled hi lo zero")
        s = semaphores(nc, ctx, "l_", "x_in0 x_in1 x_hi x_lo xcol qkv sq v ssq rn qrot krot qadd kadd tq tk "
                 "qT clamp norm hdev rsb kTa kTd sc ttr ex tr evd eva pv rl rb rbs ctx chi clo "
                 "wo xw mean hc hsq var rs hn hhi hlo ag ge u uhi ulo w2 xout out knorm nrn")

        kflat = kT[:, :, :, :].rearrange("p a b c -> p (a b c)")
        vflat = vv[:, :, :].rearrange("p a b -> p (a b)")
        qflat = qT[:, :, :].rearrange("p a b -> p (a b)")
        st_q = kflat[:, 0:KD * 3 * INNER].rearrange("p (k n) -> p k n", k=KD)
        st_1 = [kflat[:, KD * 3 * INNER:KD * 3 * INNER + 2 * HID], qflat[:, 0:2 * HID]]
        st_o = vflat[:, 0:LP * D].rearrange("p (k n) -> p k n", k=LP)
        st_2 = vflat[:, LP * D:(LP + HT) * D].rearrange("p (k n) -> p k n", k=HT)
        NR = NT * 6 * (DH // 2)
        st_r = xw[:, :, :, :].rearrange("p c a b -> p (c a b)")[:, 0:NR].rearrange("p (t s f) -> p t s f", t=NT, s=6)
        LOADS = 16

        FIRST = ("proj", "rotq", "rotk", "turnq", "turnk")
        mixed = [("proj", 0), ("rotq", 0), ("rotk", 0), ("wo", 0), ("proj", 1), ("turnq", 0), ("mean", 0),
                 ("turnk", 0), ("square", 0), ("rotq", 1), ("rotk", 1), ("deviate", 0), ("proj", 2), ("centre", 0),
                 ("turnq", 1), ("turnk", 1), ("rotq", 2), ("up", 0), ("rotk", 2), ("up", 1),
                 ("proj", 3), ("turnq", 2), ("turnk", 2), ("down", 0), ("up", 2), ("rotq", 3), ("down", 1), ("up", 3),
                 ("rotk", 3), ("down", 2), ("up", 4), ("turnq", 3), ("turnk", 3), ("down", 3), ("up", 5),
                 ("down", 4), ("down", 5)]
        assert TC == 4 and HT == 6

        def steps(q):
            return [(name, i) for name, i in mixed
                    if (q + 1 < QN if name in FIRST else q >= 0)]

        def layer_block(block, b):
            UC = TC * LP
            H2 = DH // 2
            BQ, BK, BV = 0, 1, 2
            BT = 3
            BA, BG = 4, 5
            BO = 6
            BS = 0
            BP = 3
            BC = 5
            BR = 7

            heads = lambda ap: ap.rearrange("p (h d) -> p h d", h=LH)
            halves = lambda ap: ap.rearrange("p (h a f) -> p h a f", h=LH, a=2)
            hcen = xout
            own = lambda q: xw[:, q % NC, 0, 1:CH + 1]
            prev = lambda q: xw[:, q % NC, 1, 0:CH]

            def keys(u):
                g = u // LP
                if g % NT == 0:
                    return [g % SLOTS], mask[:, P:2 * P]
                a, c = (g - 1) % SLOTS, g % SLOTS
                return ([a, c], mask[:, 0:2 * P]) if a < c else ([c, a], mask[:, P:3 * P])

            def copy_turned(eng, u):
                slots, _ = keys(u)
                k = len(slots) * P
                src = ps[:, BP + u % 2, :].rearrange("p (h k) -> p h k", h=2)[:, :, 0:k]
                dst = PT[:, u % 3, :].rearrange("p (h k) -> p h k", h=2)[:, :, 0:k]
                if u % 2:
                    return eng.activation(dst, src, ACT.Copy)
                return eng.tensor_copy(dst, src)

            groups = state.rearrange("(b s) p k n -> b s p k n", s=SB)

            @block.sync
            def _(sp):
                def load(q):
                    c = q % NC
                    src = groups[bass.ds(b, 1), q // NC, :, :, max(c * CH - 1, 0):(c + 1) * CH]
                    sp.dma_start(xw[:, c, :, 1 - min(c, 1):CH + 1], src.rearrange("b p k n -> p (b k) n")
                                 ).then_inc(s[f"x_in{c}"], 16)

                for q in range(NC):
                    load(q)
                for q in range(QN):
                    sp.wait_ge(s["xout"], KD * (q + 1))
                    sp.dma_start(groups[bass.ds(b, 1), q // NC, :, :, q % NC * CH:(q % NC + 1) * CH].rearrange(
                        "b p k n -> p (b k) n"), xout[:, :, :]).then_inc(s["out"], 16)
                    if q + NC < QN:
                        load(q + NC)
                sp.wait_ge(s["out"], 16 * QN)

            @block.tensor
            def _(pe):
                def proj(g):
                    t = g % TC
                    if t == 0:
                        pe.wait_ge(s["x_lo"], KD * (g // TC + 1))
                        if g:
                            pe.wait_ge(s["ttr"], 2 * UC * (g // TC))
                    if g:
                        pe.wait_ge(s["krot"], g)
                        pe.wait_ge(s["v"], g)
                    for i in range(3):
                        cols = slice(i * INNER, (i + 1) * INNER)
                        tok = slice(t * P, (t + 1) * P)
                        three(pe, ps[:, BQ + i, :],
                              [(xh[:, k, tok], xl[:, k, tok], Wq_hi[:, k, cols], Wq_lo[:, k, cols]) for k in range(KD)]
                              ).then_inc(s["qkv"], 1)

                def turnq(g):
                    pe.wait_ge(s["qadd"], g + 1)
                    if g:
                        pe.wait_ge(s["kTa"], g)
                        pe.wait_ge(s["kTd"], g)
                    if g and g % TC == 0:
                        pe.wait_ge(s["evd"], UC // 2 * (g // TC))
                    for j in range(LP):
                        last = pe.transpose(ps[:, BT, j * P:(j + 1) * P], t1[:, g % 2, 0, j * P:(j + 1) * P], ident[:, :])
                    last.then_inc(s["tq"], 1)

                def turnk(g):
                    pe.wait_ge(s["kadd"], g + 1)
                    pe.wait_ge(s["qT"], g + 1)
                    for j in range(LP):
                        last = pe.transpose(ps[:, BT, j * P:(j + 1) * P], t1[:, g % 2, 1, j * P:(j + 1) * P], ident[:, :])
                    last.then_inc(s["tk"], 1)

                def scores(u):
                    j, g = u % LP, u // LP
                    if u % UC == 0:
                        pe.wait_ge(s["qT"], g + TC)
                        pe.wait_ge(s["kTa"], g + TC)
                        pe.wait_ge(s["kTd"], g + TC)
                        pe.wait_ge(s["krot"], g + TC)
                        pe.wait_ge(s["v"], g + TC)
                    if u % UC >= 3:
                        pe.wait_ge(s["ttr"], 2 * (u - 2))
                    slots, _ = keys(u)
                    n = P * len(slots)
                    kview = kT[:, j, :, :].rearrange("p h (s k) -> p h s k", s=SLOTS)
                    a = slots[0]
                    if len(slots) == 1:
                        rhs = kview[:, :, a, :]
                    else:
                        rhs = kview[:, :, a:slots[1] + 1:slots[1] - a, :]
                    out = ps[:, BS + u % 3, 0:2 * n]
                    t = g % TC
                    pe.matmul(out, qT[:, j, t * P:(t + 1) * P], rhs, start=True, stop=True).then_inc(s["sc"], 1)

                def turn_p(u):
                    pe.wait_ge(s["ex"], 2 * (u + 1))
                    if u % UC >= 2:
                        pe.wait_ge(s["eva"] if u % 2 else s["evd"], u // 2)
                    elif u % UC and u > UC:
                        pe.wait_ge(s["u"], HT * (u // UC))
                    slots, _ = keys(u)
                    for h in range(2):
                        for i in range(len(slots)):
                            k = h * 2 + i
                            last = pe.transpose(ps[:, BP + u % 2, k * P:(k + 1) * P], SP[:, u % 4, h, i * P:(i + 1) * P],
                                                ident[:, :])
                    last.then_inc(s["tr"], 1)

                def weigh(u):
                    j, g = u % LP, u // LP
                    q, t = g // TC, g % TC
                    pe.wait_ge(s["eva"] if u % 2 else s["evd"], u // 2 + 1)
                    if j == 0 and t >= 2:
                        pe.wait_ge(s["ctx"], g - 1)
                    elif j == 0 and q:
                        pe.wait_ge(s["xout"] if t else s["ge"], KD * q if t else HT * q)
                    slots, _ = keys(u)
                    for i, sl in enumerate(slots):
                        for h in range(2):
                            last = pe.matmul(ps[64 * h:64 * h + 64, BC + g % 2, j * P:(j + 1) * P],
                                             vv[:, sl, (2 * j + h) * DH:(2 * j + h + 1) * DH],
                                             PT[:, u % 3, (2 * h + i) * P:(2 * h + i + 1) * P],
                                             start=(i == 0), stop=(i == len(slots) - 1), skip_group_check=True)
                    last.then_inc(s["pv"], 1)

                def spread(g):
                    pe.wait_ge(s["rl"], g + 1)
                    if g % TC:
                        pe.wait_ge(s["rbs"], g)
                    elif g:
                        pe.wait_ge(s["xout"], KD * (g // TC))
                    for j in range(LP):
                        for h in range(2):
                            last = pe.matmul(ps[64 * h:64 * h + 64, BR, j * P:(j + 1) * P],
                                             rl[:, g % 2, 2 * j + h:2 * j + h + 1].to_broadcast([P, DH]), ident[:, :],
                                             start=True, stop=True, skip_group_check=True)
                    last.then_inc(s["rb"], 1)

                def project(q):
                    pe.wait_ge(s["clo"], TC * (q + 1))
                    pe.wait_ge(s["rbs"], TC * (q + 1))
                    for m_ in range(KD):
                        f = slice(m_ * P, (m_ + 1) * P)
                        three(pe, ps[:, BO + m_, :], [(Wo_hi[:, k, f], Wo_lo[:, k, f], ah[:, k, :], al[:, k, :])
                                                      for k in range(LP)]).then_inc(s["wo"], 1)

                def mean(q):
                    pe.wait_ge(s["xw"], KD * (q + 1))
                    if q % NC:
                        pe.wait_ge(s["xcol"], (q + 1) // NC)
                    pe.wait_ge(s["eva"], UC // 2 * (q + 1))
                    for k, rhs in enumerate((own(q), prev(q))):
                        last = pe.matmul(ps[:, BA, :], ones[:, :], rhs, start=(k == 0), stop=(k == KD - 1))
                    last.then_inc(s["mean"], 1)

                def square(q):
                    pe.wait_ge(s["hsq"], q + 1)
                    for t in range(TC):
                        for k in range(KD):
                            last = pe.matmul(ps[:, BG, t:t + 1], rbs[:, k, t * P:(t + 1) * P],
                                             ones[:, 0:1], start=(k == 0), stop=(k == KD - 1))
                    last.then_inc(s["var"], 1)

                def centre(q):
                    pe.wait_ge(s["rs"], q + 1)
                    for t in range(TC):
                        last = pe.transpose(ps[:, BA, t * P:(t + 1) * P], hrs[:, q % 2, t:t + 1].to_broadcast([P, P]),
                                            ident[:, :])
                    last.then_inc(s["rsb"], 1)

                def up(q, j):
                    n, mj = HT * q + j, rows_of(j)
                    if j == 0:
                        pe.wait_ge(s["hlo"], q + 1)
                        pe.wait_ge(s["hdev"], q + 1)
                    for i, bank in ((1, BG), (0, BA)):
                        if j:
                            pe.wait_ge(s["ge"] if i else s["u"], n)
                        f = slice(i * HID + j * HW, i * HID + j * HW + mj)
                        three(pe, ps[0:mj, bank, :],
                              [(W1_hi[:, k, f], W1_lo[:, k, f], hh_[:, k, :], hl_[:, k, :]) for k in range(KD)]
                              ).then_inc(s["ag"], 1)

                def down(q, j):
                    n, mj = HT * q + j, rows_of(j)
                    pe.wait_ge(s["ulo"], n + 1)
                    if j == 0:
                        pe.wait_ge(s["xw"], KD * (q + 1))
                    for m_ in range(KD):
                        f = slice(m_ * P, (m_ + 1) * P)
                        last = three(pe, ps[:, BO + m_, :], [(W2_hi[0:mj, j, f], W2_lo[0:mj, j, f], ah[0:mj, j, :],
                                                              al[0:mj, j, :])], start=(j == 0), stop=(j == HT - 1))
                        if j == HT - 1:
                            last.then_inc(s["w2"], 1)

                for q in range(-1, QN):
                    if q >= 0:
                        for i in range(UC + 4):
                            u = q * UC + i
                            if i < UC:
                                scores(u)
                            if 2 <= i < UC + 2:
                                turn_p(u - 2)
                            if 3 <= i < UC + 3:
                                weigh(u - 3)
                            if i >= 7 and (i - 7) % LP == 0:
                                spread((u - 7) // LP)
                    for name, i in steps(q):
                        g = (q + 1) * TC + i
                        if name == "proj":
                            proj(g)
                        elif name == "turnq":
                            turnq(g)
                        elif name == "turnk":
                            turnk(g)
                        elif name == "wo":
                            project(q)
                        elif name == "mean":
                            mean(q)
                        elif name == "square":
                            square(q)
                        elif name == "centre":
                            centre(q)
                        elif name == "up":
                            up(q, i)
                        elif name == "down":
                            down(q, i)

            @block.scalar
            def _(act):
                def squares(g):
                    act.wait_ge(s["qkv"], 3 * g + 1)
                    if g:
                        act.wait_ge(s["ssq"], g)
                    act.activation(sq[:, 0:CH], ps[:, BQ, :], ACT.Square).then_inc(s["sq"], 1)
                    act.wait_ge(s["qkv"], 3 * g + 2)
                    act.activation(sq[:, CH:2 * CH], ps[:, BK, :], ACT.Square).then_inc(s["sq"], 1)
                    act.wait_ge(s["qkv"], 3 * g + 3)
                    if g >= SLOTS:
                        act.wait_ge(s["pv"], LP * (g - SLOTS + 2))
                    act.activation(vv[:, g % SLOTS, :], ps[:, BV, :], ACT.Copy).then_inc(s["v"], 1)

                def norms(g):
                    act.wait_ge(s["clamp"], g + 1)
                    act.activation(norm[:, g % 2, :], ssq[:, g % 2, :], ACT.Sqrt).then_inc(s["norm"], 1)

                def turnq(g):
                    act.wait_ge(s["tq"], g + 1)
                    t = g % TC
                    if g and t == 0:
                        act.wait_ge(s["sc"], UC * (g // TC))
                    act.activation(qT[:, :, t * P:(t + 1) * P], ps[:, BT, :].rearrange("p (j k) -> p j k", j=LP),
                                   ACT.Copy).then_inc(s["qT"], 1)

                def turnk(g):
                    act.wait_ge(s["tk"], g + 1)
                    sl = g % SLOTS
                    act.activation(kT[0:64, :, 0, sl * P:(sl + 1) * P],
                                   ps[0:64, BT, :].rearrange("p (j k) -> p j k", j=LP), ACT.Copy).then_inc(s["kTa"], 1)

                def exps(u):
                    j, g = u % LP, u // LP
                    slots, _ = keys(u)
                    n = P * len(slots)
                    if j == 0 and g >= 2:
                        act.wait_ge(s["rl"], g - 1)
                    for h in range(2):
                        act.wait_ge(s["ttr"], 2 * u + h + 1)
                        act.activation(SP[:, u % 4, h, 0:n], SP[:, u % 4, h, 0:n], ACT.Exp, bias=mn[:, u % 4, h:h + 1],
                                       scale=-1.0, accum_out=ls[:, g % 2, 2 * j + h:2 * j + h + 1]).then_inc(s["ex"], 1)

                def copy_p(u):
                    act.wait_ge(s["tr"], u + 1)
                    if u >= 3:
                        act.wait_ge(s["pv"], u - 2)
                    copy_turned(act, u).then_inc(s["eva"], 1)

                def copy_r(g):
                    act.wait_ge(s["rb"], g + 1)
                    if g >= 2:
                        act.wait_ge(s["ctx"], g - 1)
                    if g >= TC and g % TC < 2:
                        act.wait_ge(s["u"], HT * (g // TC))
                    act.activation(rbs[:, g % 2, :], ps[:, BR, :], ACT.Copy).then_inc(s["rbs"], 1)

                def square(q):
                    act.wait_ge(s["hc"], KD * (q + 1))
                    act.wait_ge(s["ctx"], TC * (q + 1))
                    act.activation(rbs[:, :, :], hcen[:, :, :], ACT.Square).then_inc(s["hsq"], 1)

                def deviate(q):
                    act.wait_ge(s["var"], q + 1)
                    act.activation(hdev[:, q % 2, :], ps[:, BG, 0:TC], ACT.Sqrt, bias=eps[:, :]).then_inc(s["hdev"], 1)

                def up(q, j):
                    n, mj = HT * q + j, rows_of(j)
                    act.wait_ge(s["ag"], 2 * n + 1)
                    if j >= 2:
                        act.wait_ge(s["u"], n - 1)
                    act.activation(rbs[0:mj, j % 2, :], ps[0:mj, BG, :], ACT.Gelu,
                                   bias=b1c[0:mj, 1, j:j + 1]).then_inc(s["ge"], 1)

                for q in range(-1, QN):
                    if q >= 0:
                        for i in range(UC + 4):
                            u = q * UC + i
                            if i < UC:
                                exps(u)
                            if 2 <= i < UC + 2 and (i - 2) % 2:
                                copy_p(u - 2)
                            if i >= 7 and (i - 7) % LP == 0:
                                copy_r((u - 7) // LP)
                    for name, i in steps(q):
                        g = (q + 1) * TC + i
                        if name == "proj":
                            squares(g)
                        elif name == "rotq":
                            norms(g)
                        elif name == "turnq":
                            turnq(g)
                        elif name == "turnk":
                            turnk(g)
                        elif name == "square":
                            square(q)
                        elif name == "deviate":
                            deviate(q)
                        elif name == "up":
                            up(q, i)

            @block.vector
            def _(dve):
                def split(q, part):
                    if part == 0:
                        dve.wait_ge(s[f"x_in{q % NC}"], 16 * (q // NC + 1))
                        if q:
                            dve.wait_ge(s["qkv"], 3 * TC * q)
                        for k, src in enumerate((own(q), prev(q))):
                            dve.tensor_copy(xh[:, k, :], src).then_inc(s["x_hi"], 1)
                    else:
                        dve.wait_ge(s["x_hi"], KD * (q + 1))
                        for k, src in enumerate((own(q), prev(q))):
                            dve.tensor_tensor(xl[:, k, :], src, xh[:, k, :], ALU.subtract).then_inc(s["x_lo"], 1)

                C = lambda i, g: rotC[:, i, g % NT:g % NT + 1, :].to_broadcast([P, LH, DH])
                S = lambda i, g, a: rotS[:, i, g % NT:g % NT + 1, a * H2:(a + 1) * H2].to_broadcast([P, LH, H2])

                def rotq(g):
                    q = ps[:, BQ, :]
                    dve.wait_ge(s["sq"], 2 * g + 2)
                    dve.tensor_reduce(ssq[:, g % 2, :], sq[:, :].rearrange("p (h d) -> p h d", d=DH), AX_X,
                                      ALU.add).then_inc(s["ssq"], 1)
                    dve.wait_ge(s["ssq"], g + 1)
                    dve.tensor_scalar(ssq[:, g % 2, :], ssq[:, g % 2, :], 1e-24, None, ALU.max).then_inc(s["clamp"], 1)
                    if g >= 2:
                        dve.wait_ge(s["tk"], g - 1)
                    dve.tensor_tensor(heads(t1[:, g % 2, 0, :]), heads(q), C(0, g), ALU.mult).then_inc(s["qrot"], 1)
                    if g:
                        dve.wait_ge(s["qadd"], g)
                    for a in range(2):
                        dve.tensor_tensor(halves(t2[:, 0, :])[:, :, a, :], halves(q)[:, :, 1 - a, :], S(0, g, a),
                                          ALU.mult).then_inc(s["qrot"], 1)

                def rotk(g):
                    k = ps[:, BK, :]
                    dve.wait_ge(s["norm"], g + 1)
                    dve.reciprocal(rn[:, g % 2, :], norm[:, g % 2, :]).then_inc(s["rn"], 1)
                    dve.wait_ge(s["rn"], g + 1)
                    dve.tensor_scalar(nrn[:, g % NT, :], rn[:, g % 2, 0:LH], -8.0, None, ALU.mult).then_inc(s["nrn"], 1)
                    dve.tensor_tensor(heads(kn[:, :]), heads(k), rn[:, g % 2, LH:2 * LH].unsqueeze(2).to_broadcast(
                        [P, LH, DH]), ALU.mult).then_inc(s["krot"], 1)
                    dve.wait_ge(s["krot"], g + 1)
                    dve.tensor_tensor(heads(t1[:, g % 2, 1, :]), heads(kn[:, :]), C(1, g), ALU.mult).then_inc(s["knorm"], 1)
                    if g:
                        dve.wait_ge(s["kadd"], g)
                    for a in range(2):
                        dve.tensor_tensor(halves(t2[:, 1, :])[:, :, a, :], halves(kn[:, :])[:, :, 1 - a, :], S(1, g, a),
                                          ALU.mult).then_inc(s["knorm"], 1)

                def turnk(g):
                    dve.wait_ge(s["tk"], g + 1)
                    sl = g % SLOTS
                    dve.tensor_copy(kT[64:128, :, 1, sl * P:(sl + 1) * P],
                                    ps[64:128, BT, :].rearrange("p (j k) -> p j k", j=LP)).then_inc(s["kTd"], 1)

                def masked(u):
                    j, g = u % LP, u // LP
                    slots, mk = keys(u)
                    n = P * len(slots)
                    dve.wait_ge(s["sc"], u + 1)
                    if u >= 4:
                        dve.wait_ge(s["tr"], u - 3)
                    if j == 0:
                        dve.wait_ge(s["nrn"], g + 1)
                    for h in range(2):
                        dve.tensor_tensor_reduce(SP[:, u % 4, h, 0:n], ps[:, BS + u % 3, h * n:(h + 1) * n], mk,
                                                 nrn[:, g % NT, 2 * j + h:2 * j + h + 1], BIG, ALU.add, ALU.min,
                                                 mn[:, u % 4, h:h + 1]).then_inc(s["ttr"], 1)

                def copy_p(u):
                    dve.wait_ge(s["tr"], u + 1)
                    if u >= 3:
                        dve.wait_ge(s["pv"], u - 2)
                    copy_turned(dve, u).then_inc(s["evd"], 1)

                def recip(g):
                    dve.wait_ge(s["ex"], 2 * LP * (g + 1))
                    if g >= 2:
                        dve.wait_ge(s["rb"], g - 1)
                    dve.reciprocal(rl[:, g % 2, :], ls[:, g % 2, :]).then_inc(s["rl"], 1)

                def normalise(g):
                    q, t = g // TC, g % TC
                    dve.wait_ge(s["pv"], LP * (g + 1))
                    dve.wait_ge(s["rbs"], g + 1)
                    if g >= 2:
                        dve.wait_ge(s["clo"], g - 1)
                    if q and t == 0:
                        dve.wait_ge(s["w2"], KD * q)
                    dve.tensor_tensor(ctxf[:, g % 2, :], ps[:, BC + g % 2, :], rbs[:, g % 2, :], ALU.mult).then_inc(s["ctx"], 1)
                    dve.wait_ge(s["ctx"], g + 1)
                    dve.tensor_copy(ah[:, 0:LP, t * P:(t + 1) * P], ctxf[:, g % 2, :].rearrange("p (j k) -> p j k", j=LP)
                                    ).then_inc(s["chi"], 1)

                def residual(q):
                    for k in range(KD):
                        dve.wait_ge(s["wo"], KD * q + k + 1)
                        row = xw[:, q % NC, k, 1:CH + 1]
                        dve.tensor_tensor(row, ps[:, BO + k, :], row, ALU.add).then_inc(s["xw"], 1)
                    dve.wait_ge(s["xw"], KD * (q + 1))
                    if q % NC < NC - 1:
                        dve.tensor_copy(xw[:, q % NC + 1, 1, 0:1], xw[:, q % NC, 1, CH:CH + 1]).then_inc(s["xcol"], 1)

                def mean(q):
                    dve.wait_ge(s["mean"], q + 1)
                    if q:
                        dve.wait_ge(s["out"], 16 * q)
                    for k, src in enumerate((own(q), prev(q))):
                        dve.tensor_tensor(hcen[:, k, :], src, ps[:, BA, :], ALU.subtract).then_inc(s["hc"], 1)

                def deviate(q):
                    dve.wait_ge(s["hdev"], q + 1)
                    dve.reciprocal(hrs[:, q % 2, :], hdev[:, q % 2, :]).then_inc(s["rs"], 1)

                def centre(q):
                    dve.wait_ge(s["rsb"], q + 1)
                    dve.tensor_tensor(hcen[:, :, :], hcen[:, :, :], ps[:, BA:BA + 1, :].to_broadcast([P, KD, CH]),
                                      ALU.mult).then_inc(s["hn"], 1)
                    dve.wait_ge(s["hn"], q + 1)
                    if q:
                        dve.wait_ge(s["ag"], 2 * HT * q)
                    dve.tensor_copy(hh_[:, :, :], hcen[:, :, :]).then_inc(s["hhi"], 1)
                    dve.wait_ge(s["hhi"], q + 1)
                    dve.tensor_tensor(hl_[:, :, :], hcen[:, :, :], hh_[:, :, :], ALU.subtract).then_inc(s["hlo"], 1)

                def up(q, j):
                    n, mj = HT * q + j, rows_of(j)
                    dve.wait_ge(s["ag"], 2 * n + 2)
                    dve.wait_ge(s["ge"], n + 1)
                    if j >= 2:
                        dve.wait_ge(s["ulo"], n - 1)
                    elif j == 0:
                        dve.wait_ge(s["clo"], TC * (q + 1))
                    dve.scalar_tensor_tensor(out=ctxf[0:mj, j % 2, :], in0=ps[0:mj, BA, :],
                                             scalar=b1c[0:mj, 0, j:j + 1], in1=rbs[0:mj, j % 2, :], op0=ALU.add,
                                             op1=ALU.mult).then_inc(s["u"], 1)
                    dve.wait_ge(s["u"], n + 1)
                    dve.tensor_copy(ah[0:mj, j, :], ctxf[0:mj, j % 2, :]).then_inc(s["uhi"], 1)

                def output(q):
                    for k in range(KD):
                        dve.wait_ge(s["w2"], KD * q + k + 1)
                        dve.scalar_tensor_tensor(out=xout[:, k, :], in0=ps[:, BO + k, :], scalar=b2c[:, k:k + 1],
                                                 in1=xw[:, q % NC, k, 1:CH + 1], op0=ALU.add,
                                                 op1=ALU.add).then_inc(s["xout"], 1)

                split(0, 0)
                split(0, 1)
                for q in range(-1, QN):
                    if q >= 0:
                        for i in range(UC + 4):
                            u = q * UC + i
                            if i < UC:
                                masked(u)
                            if 2 <= i < UC + 2 and (i - 2) % 2 == 0:
                                copy_p(u - 2)
                            if i >= 4 and (i - 4) % LP == 0:
                                recip((u - 4) // LP)
                            if i >= 7 and (i - 7) % LP == 0:
                                normalise((u - 7) // LP)
                            if i in (9, 13) and q + 1 < QN:
                                split(q + 1, i // 13)
                    for name, i in steps(q):
                        g = (q + 1) * TC + i
                        if name == "rotq":
                            rotq(g)
                        elif name == "rotk":
                            rotk(g)
                        elif name == "turnk":
                            turnk(g)
                        elif name == "wo":
                            residual(q)
                        elif name == "mean":
                            mean(q)
                        elif name == "deviate":
                            deviate(q)
                        elif name == "centre":
                            centre(q)
                        elif name == "up":
                            up(q, i)
                        elif name == "down" and i == HT - 1:
                            output(q)

            @block.gpsimd
            def _(pool):
                for q in range(-1, QN):
                    if q >= 0:
                        for t in range(TC):
                            g = q * TC + t
                            pool.wait_ge(s["chi"], g + 1)
                            cols = slice(t * P, (t + 1) * P)
                            pool.tensor_tensor(al[:, 0:LP, cols], ctxf[:, g % 2, :].rearrange("p (j k) -> p j k", j=LP),
                                               ah[:, 0:LP, cols], ALU.subtract).then_inc(s["clo"], 1)
                    for name, i in steps(q):
                        g, n = (q + 1) * TC + i, HT * q + i
                        if name == "rotq":
                            pool.wait_ge(s["qrot"], 3 * (g + 1))
                            pool.tensor_tensor(t1[:, g % 2, 0, :], t1[:, g % 2, 0, :], t2[:, 0, :], ALU.add
                                               ).then_inc(s["qadd"], 1)
                        elif name == "rotk":
                            pool.wait_ge(s["knorm"], 3 * (g + 1))
                            pool.tensor_tensor(t1[:, g % 2, 1, :], t1[:, g % 2, 1, :], t2[:, 1, :], ALU.add
                                               ).then_inc(s["kadd"], 1)
                        elif name == "up":
                            mj = rows_of(i)
                            pool.wait_ge(s["uhi"], n + 1)
                            pool.tensor_tensor(al[0:mj, i, :], ctxf[0:mj, i % 2, :], ah[0:mj, i, :], ALU.subtract
                                               ).then_inc(s["ulo"], 1)

        with nc.Fori(0, DEPTH) as l:
            one = lambda t: t[bass.ds(l, 1)]
            with nc.Block() as block:
                @block.sync
                def _(sp):
                    with nc.allow_non_contiguous_dma(reason="bias columns"):
                        sp.dma_start(st_q, one(wqkv).rearrange("l (k p) n -> p (l k) n", p=P)).then_inc(w["load"], 16)
                        for k in range(KD):
                            sp.dma_start(st_1[k], one(w1)[:, k * P:(k + 1) * P].rearrange("l p n -> (l p) n")
                                         ).then_inc(w["load"], 16)
                        sp.dma_start(st_o, one(wo).rearrange("l (k p) n -> p (l k) n", p=P)).then_inc(w["load"], 16)
                        sp.dma_start(st_2[0:HW, 0:HT - 1, :], one(w2)[:, 0:(HT - 1) * HW].rearrange(
                            "l (k p) n -> p (l k) n", p=HW)).then_inc(w["load"], 16)
                        sp.dma_start(st_2[0:HREM, HT - 1, :], one(w2)[:, (HT - 1) * HW:HID].rearrange(
                            "l p n -> (l p) n")).then_inc(w["load"], 16)
                        sp.dma_start(st_r, rot).then_inc(w["load"], 16)
                        for i in range(2):
                            sp.dma_start(b1c[0:HW, i, 0:HT - 1], one(b1)[:, i * HID:i * HID + (HT - 1) * HW].rearrange(
                                "l (k p) -> p (l k)", p=HW)).then_inc(w["load"], 16)
                            sp.dma_start(b1c[0:HREM, i, HT - 1:HT], one(b1)[
                                :, i * HID + (HT - 1) * HW:(i + 1) * HID].rearrange("l p -> p l")).then_inc(w["load"], 16)
                        for dst, src in ((b2c, b2), (lg, ln_g), (lb, ln_b)):
                            sp.dma_start(dst[:, :], one(src).rearrange("l (k p) -> p (l k)", p=P)).then_inc(w["load"], 16)
                        for i, src in enumerate((q_scale, k_scale)):
                            sp.dma_start(qsc[:, i, :], one(src).rearrange("l d -> (l d)").partition_broadcast(P)
                                         ).then_inc(w["load"], 16)

                @block.gpsimd
                def _(pool):
                    pool.memset(mask[:, :], 0.0).then_inc(w["mask"], 1)
                    pool.wait_ge(w["mask"], 1)
                    for k, sign in enumerate((1, -1, 1)):
                        pool.affine_select(out=mask[:, k * P:(k + 1) * P], in_=mask[:, k * P:(k + 1) * P],
                                           compare_op=ALU.is_ge, fill=NEG, base=0, pattern=[[sign, P]],
                                           channel_multiplier=-sign).then_inc(w["masked"], 1)
                    pool.wait_ge(w["load"], 16 * LOADS)
                    H2 = DH // 2
                    for i in range(2):
                        for h in range(2):
                            own = qsc[:, i:i + 1, h * H2:(h + 1) * H2].to_broadcast([P, NT, H2])
                            other = qsc[:, i:i + 1, (1 - h) * H2:(2 - h) * H2].to_broadcast([P, NT, H2])
                            pool.tensor_tensor(rotC[:, i, :, h * H2:(h + 1) * H2], st_r[:, :, 3 * i, :], own,
                                               ALU.mult).then_inc(w["tab"], 1)
                            pool.tensor_tensor(rotS[:, i, :, h * H2:(h + 1) * H2], st_r[:, :, 3 * i + 1 + h, :],
                                               other, ALU.mult).then_inc(w["tab"], 1)
                    pool.wait_ge(w["tab"], 8)
                    pool.memset(xw[:, 0, :, 0:1], 0.0).then_inc(w["zero"], 1)
                    pool.wait_ge(w["lo"], 4)
                    pool.wait_ge(w["zero"], 1)
                    for a in range(2):
                        pool.memset(kT[64 - 64 * a:128 - 64 * a, :, a, :], 0.0).then_inc(w["zero"], 1)
                        pool.wait_ge(w["zero"], 2 + a)
                    pool.wait_ge(w["masked"], 3)

                @block.tensor
                def _(pe):
                    pe.wait_ge(w["load"], 16 * LOADS)
                    for i in range(2):
                        for j in range(HT):
                            f0, m = i * HID + j * HW, rows_of(j)
                            for k in range(KD):
                                last = pe.matmul(ps[0:m, 0, i * HT + j:i * HT + j + 1], st_1[k][:, f0:f0 + m],
                                                 lb[:, k:k + 1], start=(k == 0), stop=(k == KD - 1))
                    last.then_inc(w["bias"], 1)

                @block.vector
                def _(dve):
                    dve.wait_ge(w["load"], 16 * LOADS)
                    dve.wait_ge(w["bias"], 1)
                    bias = ps[:, 0, 0:2 * HT].rearrange("p (i j) -> p i j", i=2)
                    dve.tensor_tensor(b1c[0:HW, :, 0:HT - 1], b1c[0:HW, :, 0:HT - 1], bias[0:HW, :, 0:HT - 1], ALU.add
                                      ).then_inc(w["biased"], 1)
                    dve.tensor_tensor(b1c[0:HREM, :, HT - 1], b1c[0:HREM, :, HT - 1], bias[0:HREM, :, HT - 1],
                                      ALU.add).then_inc(w["biased"], 1)
                    for k in range(KD):
                        dve.tensor_scalar(st_1[k], st_1[k], lg[:, k:k + 1], None, ALU.mult).then_inc(w["scaled"], 1)
                    n_hi = 0
                    parts = [(Wq_hi[:, :, :], Wq_lo[:, :, :], st_q)]
                    parts += [(W1_hi[:, k, :], W1_lo[:, k, :], st_1[k]) for k in range(KD)]
                    parts += [(Wo_hi[:, :, :], Wo_lo[:, :, :], st_o)]
                    parts += [(W2_hi[0:HW, 0:HT - 1, :], W2_lo[0:HW, 0:HT - 1, :], st_2[0:HW, 0:HT - 1, :])]
                    parts += [(W2_hi[0:HREM, HT - 1, :], W2_lo[0:HREM, HT - 1, :], st_2[0:HREM, HT - 1, :])]
                    dve.wait_ge(w["scaled"], KD)
                    for hi, lo, src in parts:
                        dve.tensor_copy(hi, src).then_inc(w["hi"], 1)
                        n_hi += 1
                        dve.wait_ge(w["hi"], n_hi)
                        dve.tensor_tensor(lo, src, hi, ALU.subtract).then_inc(w["lo"], 1)
                    dve.wait_ge(w["lo"], len(parts))
                    dve.wait_ge(w["biased"], 2)
            clear(nc, w)

            with nc.Fori(0, B // SB) as b:
                with nc.Block() as block:
                    layer_block(block, b)
                clear(nc, s)


def stage_g(nc, x, A, xnorm, state, out, ident, ps):
    Wq, Wkv_down, Wk_up, Wv_up, Wout = A
    with ExitStack() as ctx:
        sb = lambda n, sh, dt=F32: ctx.enter_context(nc.sbuf_tensor(n, sh, dt))
        two = lambda n, sh: (sb(n + "_hi", sh, F32R), sb(n + "_lo", sh, F32R))
        Gh, Gl = two("g_wq", [P, KD, GH * DH])
        Oh, Ol = two("g_wo", [P, GP, D])
        Kh, Kl = two("g_wk", [P, KD, 2 * DH])
        mask = sb("g_mask", [P, N])
        xtok = sb("g_xtok", [P, NT, D])
        xnh, xnl = two("g_xn2", [P, KD, N])
        fT = sb("g_fT", [P, KD, N])
        lath, latl = two("g_lat", [P, N])
        latV = sb("g_latV", [P, NT, DH])
        qst = sb("g_q", [P, GH, CH], F32R)
        SP = sb("g_sp", [P, 3, 4, N])
        xn = SP[:, 2, 0:2, :].rearrange("p k n -> p (k n)").rearrange("p (k n) -> p k n", k=KD)
        latf = SP[0:DH, 2, 2, :]
        PT = sb("g_pt", [P, 4, CH])
        rbs = sb("g_rbs", [P, 2, 2 * P])
        ctxf = sb("g_ctxf", [P, 2, 2 * P])
        ch, cl = two("g_ctx", [P, GP, CH])
        mn = sb("g_mn", [P, 3, 4])
        ls = sb("g_ls", [P, 3, 4])
        rl = sb("g_rl", [P, 2, 4])

        w = semaphores(nc, ctx, "gw_", "load mask tq tk g o hi lo copied khi klo ghi glo")
        s = semaphores(nc, ctx, "g_", "x_in xn_in0 xn_in1 xhi xlo f_in silu lat lathi latf latlo "
                 "vt v q qhi qlo sc ttr ex tr eva evd pv rl rb rbs ctx chi clo wo prod back y out")

        sflat = SP[:, :, :, :].rearrange("p a b c -> p (a b c)")
        xflat = xtok[:, :, :].rearrange("p a b -> p (a b)")
        HD_ = GH * DH
        wq_s = sflat[:, 0:KD * HD_].rearrange("p (k n) -> p k n", k=KD)
        wk_s = sflat[0:DH, 2048:2048 + HD_]
        wv_s = sflat[0:DH, 3072:3072 + HD_]
        wo_s = sflat[:, 4096:4096 + GP * D].rearrange("p (j n) -> p j n", j=GP)
        wqT = sflat[:, 6144:6144 + GP * D].rearrange("p (j n) -> p j n", j=GP)
        wkT = xflat[:, 0:GP * DH].rearrange("p (j n) -> p j n", j=GP)
        wvT = xflat[:, 512:512 + GP * DH].rearrange("p (j n) -> p j n", j=GP)
        kd_s = xflat[:, 1024:1024 + KD * DH].rearrange("p (k n) -> p k n", k=KD)

        with nc.Block() as block:
            @block.sync
            def _(sp):
                for dst, src in ((wq_s, Wq.rearrange("(k p) h d -> p k (h d)", p=P)),
                                 (wk_s, Wk_up.rearrange("c h d -> c (h d)")),
                                 (wv_s, Wv_up.rearrange("c h d -> c (h d)")),
                                 (wo_s, Wout.rearrange("h d o -> (h d) o").rearrange("(j p) o -> p j o", p=P)),
                                 (kd_s, Wkv_down.rearrange("(k p) c -> p k c", p=P))):
                    sp.dma_start(dst, src).then_inc(w["load"], 16)

            @block.gpsimd
            def _(pool):
                pool.memset(mask[:, :], 0.0).then_inc(w["mask"], 1)
                pool.wait_ge(w["mask"], 1)
                pool.affine_select(out=mask[:, N - P:N], in_=mask[:, N - P:N], compare_op=ALU.is_ge, fill=NEG,
                                   base=0, pattern=[[-1, P]], channel_multiplier=1).then_inc(w["mask"], 1)
                pool.wait_ge(w["mask"], 2)

            @block.tensor
            def _(pe):
                pe.wait_ge(w["load"], 16 * 5)
                for j in range(GP):
                    for k in range(KD):
                        last = pe.transpose(ps[:, j // 2, (j % 2) * D + k * P:(j % 2) * D + (k + 1) * P],
                                            wq_s[:, k, j * P:(j + 1) * P], ident[:, :])
                last.then_inc(w["tq"], 1)
                for bank, src in ((4, wk_s), (5, wv_s)):
                    for j in range(GP):
                        last = pe.transpose(ps[:, bank, j * DH:(j + 1) * DH], src[:, j * P:(j + 1) * P],
                                            ident[0:DH, 0:DH])
                    last.then_inc(w["tk"], 1)
                pe.wait_ge(w["copied"], 6)
                for k in range(KD):
                    for a in range(2):
                        for j in range(GP):
                            last = pe.matmul(ps[:, 2 * k + a, j * DH:(j + 1) * DH],
                                             wqT[64 * a:64 * a + 64, j, k * P:(k + 1) * P],
                                             wkT[64 * a:64 * a + 64, j, :], start=True, stop=True)
                        last.then_inc(w["g"], 1)
                pe.wait_ge(w["glo"], 4)
                for a in range(2):
                    for j in range(GP):
                        last = pe.matmul(ps[64 * a:64 * a + 64, 4 * a + j // 2, (j % 2) * D:(j % 2 + 1) * D],
                                         wvT[64 * a:64 * a + 64, j, :], wo_s[64 * a:64 * a + 64, j, :],
                                         start=True, stop=True)
                    last.then_inc(w["o"], 1)

            @block.vector
            def _(dve):
                dve.wait_ge(w["load"], 16 * 5)
                for i in range(2):
                    dve.tensor_copy(Kh[:, :, i * DH:(i + 1) * DH], kd_s).then_inc(w["khi"], 1)
                dve.wait_ge(w["khi"], 2)
                for i in range(2):
                    dve.tensor_tensor(Kl[:, :, i * DH:(i + 1) * DH], kd_s, Kh[:, :, i * DH:(i + 1) * DH],
                                      ALU.subtract).then_inc(w["klo"], 1)
                dve.wait_ge(w["tq"], 1)
                for i in range(4):
                    dve.tensor_copy(wqT[:, 2 * i:2 * i + 2, :], ps[:, i, :].rearrange("p (j n) -> p j n", j=2)
                                    ).then_inc(w["copied"], 1)
                for i, dst in enumerate((wkT, wvT)):
                    dve.wait_ge(w["tk"], i + 1)
                    dve.tensor_copy(dst, ps[:, 4 + i, :].rearrange("p (j n) -> p j n", j=GP)).then_inc(w["copied"], 1)
                for k in range(KD):
                    for a in range(2):
                        i = 2 * k + a
                        dve.wait_ge(w["g"], i + 1)
                        view = lambda t: t[:, k, :].rearrange("p (j a n) -> p j a n", j=GP, a=2)[:, :, a, :]
                        src = ps[:, i, :].rearrange("p (j n) -> p j n", j=GP)
                        dve.tensor_scalar(view(Gh), src, DH ** -0.5, None, ALU.mult).then_inc(w["ghi"], 1)
                        dve.wait_ge(w["ghi"], i + 1)
                        dve.scalar_tensor_tensor(out=view(Gl), in0=src, scalar=DH ** -0.5, in1=view(Gh),
                                                 op0=ALU.mult, op1=ALU.subtract).then_inc(w["glo"], 1)
                for a in range(2):
                    dve.wait_ge(w["o"], a + 1)
                    rows = slice(64 * a, 64 * a + 64)
                    for i in range(4):
                        src = ps[rows, 4 * a + i, :].rearrange("p (j n) -> p j n", j=2)
                        dve.tensor_copy(Oh[rows, 2 * i:2 * i + 2, :], src).then_inc(w["hi"], 1)
                        dve.wait_ge(w["hi"], 4 * a + i + 1)
                        dve.tensor_tensor(Ol[rows, 2 * i:2 * i + 2, :], src, Oh[rows, 2 * i:2 * i + 2, :],
                                          ALU.subtract).then_inc(w["lo"], 1)
                dve.wait_ge(w["lo"], 8)
                dve.wait_ge(w["klo"], 2)
        clear(nc, w)

        UQ = GH // 4
        UC = TC * UQ
        UU = NC * UC
        tile_of = lambda u: u // UC * TC + u % TC
        tiles_of = lambda u: tile_of(u) + 1
        first = [sum(tiles_of(v) for v in range(u)) for u in range(UU + 1)]
        BT, NB, BC = 4, 3, 7
        place = lambda h: (h % 2) * 2 + h // 2
        chunk = lambda c: slice(c * CH, (c + 1) * CH)

        order = [("queries", 0, 0)]
        for u in range(UU + 3):
            new, v = u < UU, u - 2
            size = tiles_of(v) if 0 <= v < UU else 0
            late = tiles_of(v - 1) if v >= 1 else 0
            if u > UC and u % UC == 3 and new:
                order += [("wout", u // UC - 1, 0)]
            if u > UC and u % UC == 4 and new:
                order += [("back", u // UC - 1, 0)]
            order += [("scores", u, 0)] * new
            order += [("weigh", v - 1, late - 2)] * (late >= 2)
            order += [("turn", v, 0)] * (size >= 1)
            order += [("scores", u, 1)] * new
            order += [("weigh", v - 1, late - 1), ("finish", v - 1, 0)] * (late >= 1)
            if new and u % TC == TC - 1 and u + 1 < UU:
                order += [("queries", u // TC + 1, 0)]
            order += [("turn", v, 1)] * (size >= 2)
            order += [("spread", v, 0)] * (size >= 1)
            order += [("scores", u, 2)] * new
            order += [("turn", v, 2)] * (size >= 3)
            order += [("scores", u, 3)] * new
            for k in range(2, size):
                order += [("turn", v, k)] * (k > 2) + [("weigh", v, k - 2)]
        order += [("wout", NC - 1, 0), ("back", NC - 1, 0)]

        done = {"scores": lambda u, h: ("ttr", 4 * u + h + 1), "queries": lambda n, _: ("qlo", 4 * (n + 1)),
                "wout": lambda c, _: ("prod", KD * (c + 1)), "back": lambda c, _: ("y", 2 * (c + 1))}
        ring = [step for step in order if step[0] in done]
        pair = {step: 2 * (r % 2) for r, step in enumerate(ring)}
        free = {step: done[ring[r - 2][0]](*ring[r - 2][1:]) for r, step in enumerate(ring) if r >= 2}

        def copied(n):
            return ("eva", n // 2 + 1) if n % 2 else ("evd", n // 2 + 1)

        with nc.Fori(0, B) as b:
            with nc.Block() as block:
                @block.sync
                def _(sp):
                    for c in range(NC):
                        sp.dma_start(xn[:, :, chunk(c)], xnorm[bass.ds(b, 1), :, :, chunk(c)].rearrange(
                            "b p k n -> p (b k) n")).then_inc(s[f"xn_in{c}"], 16)
                    sp.dma_start(fT[:, :, :], state[bass.ds(b, 1)].rearrange("b p k n -> p (b k) n")
                                 ).then_inc(s["f_in"], 16)
                    sp.dma_start(xtok[:, :, :], x[bass.ds(b, 1)].rearrange("b (t p) d -> p (b t) d", p=P)
                                 ).then_inc(s["x_in"], 16)
                    for c in range(NC):
                        sp.wait_ge(s["y"], 2 * (c + 1))
                        sp.dma_start(out[bass.ds(b, 1), chunk(c)].rearrange("b (t p) d -> p (b t) d", p=P),
                                     xtok[:, c * TC:(c + 1) * TC, :]).then_inc(s["out"], 16)
                    sp.wait_ge(s["out"], 16 * NC)

                @block.tensor
                def _(pe):
                    for c in range(NC):
                        pe.wait_ge(s["xlo"], KD * (c + 1))
                        three(pe, ps[:, 4 + c, :], [(Kh[:, k, :], Kl[:, k, :], xnh[:, k, chunk(c)],
                                                     xnl[:, k, chunk(c)]) for k in range(KD)]).then_inc(s["lat"], 1)

                    def latents_by_token():
                        pe.wait_ge(s["latf"], NC)
                        for t in range(NT):
                            last = pe.transpose(ps[:, 6, t * DH:(t + 1) * DH], latf[:, t * P:(t + 1) * P],
                                                ident[0:DH, 0:DH])
                        last.then_inc(s["vt"], 1)

                    def queries(n, bank):
                        c, group = n // UQ, n % UQ
                        for i in range(2):
                            j = 2 * group + i
                            three(pe, ps[:, bank + i, :], [(Gh[:, k, j * P:(j + 1) * P], Gl[:, k, j * P:(j + 1) * P],
                                                            xnh[:, k, chunk(c)], xnl[:, k, chunk(c)])
                                                           for k in range(KD)]).then_inc(s["q"], 1)

                    def scores(u, h, bank):
                        n = P * tiles_of(u)
                        if u % TC == 0 and h == 0:
                            pe.wait_ge(s["qlo"], 4 * (u // TC + 1))
                            pe.wait_ge(s["latlo"], NC)
                        head, tok = 4 * (u // TC % UQ) + h, slice(u % TC * P, (u % TC + 1) * P)
                        for k in range(-(-n // CH)):
                            cols = slice(k * CH, max(min(n, (k + 1) * CH), k * CH + 2 * P))
                            o = ps[:, bank + k, 0:cols.stop - cols.start]
                            pe.matmul(o, qst[:, head, tok], lath[:, cols], start=True, stop=False)
                            last = pe.matmul(o, qst[:, head, tok], latl[:, cols], start=False, stop=True)
                        last.then_inc(s["sc"], 1)

                    def turn(u, k):
                        n = first[u] + k
                        if k == 0:
                            pe.wait_ge(s["ex"], 4 * (u + 1))
                            if u == 0:
                                pe.wait_ge(s["v"], 1)
                        if n >= NB:
                            name, value = copied(n - NB)
                            pe.wait_ge(s[name], value)
                        for h in range(4):
                            c0 = place(h) * P
                            last = pe.transpose(ps[:, BT + n % NB, c0:c0 + P], SP[:, u % 3, h, k * P:(k + 1) * P],
                                                ident[:, :])
                        last.then_inc(s["tr"], 1)

                    def weigh(u, k):
                        n = first[u] + k
                        name, value = copied(n)
                        pe.wait_ge(s[name], value)
                        if k == 0:
                            pe.wait_ge(s["rbs"], u + 1)
                        for a in range(2):
                            last = pe.matmul(ps[64 * a:64 * a + 64, BC, 0:2 * P], latV[:, k, :],
                                             PT[:, n % 4, a * 2 * P:(a + 1) * 2 * P], start=(k == 0),
                                             stop=(k == tiles_of(u) - 1), skip_group_check=True)
                        last.then_inc(s["pv"], 1)

                    def spread(u):
                        pe.wait_ge(s["rl"], u + 1)
                        if u:
                            pe.wait_ge(s["ctx"], u)
                        for j in range(2):
                            for h in range(2):
                                last = pe.matmul(ps[64 * h:64 * h + 64, BC, (2 + j) * P:(3 + j) * P],
                                                 rl[:, u % 2, 2 * j + h:2 * j + h + 1].to_broadcast([P, DH]),
                                                 ident[:, :], start=True, stop=True, skip_group_check=True)
                        last.then_inc(s["rb"], 1)

                    def wout(c, bank):
                        pe.wait_ge(s["clo"], UC * (c + 1))
                        for m in range(KD):
                            f = slice(m * P, (m + 1) * P)
                            three(pe, ps[:, bank + m, :], [(Oh[:, j, f], Ol[:, j, f], ch[:, j, :], cl[:, j, :])
                                                           for j in range(GP)]).then_inc(s["wo"], 1)

                    def back(c, bank):
                        pe.wait_ge(s["prod"], KD * (c + 1))
                        for t in range(TC):
                            for m in range(KD):
                                last = pe.transpose(ps[:, bank + t // 2, (t % 2) * D + m * P:(t % 2) * D + (m + 1) * P],
                                                    fT[:, m, c * CH + t * P:c * CH + (t + 1) * P], ident[:, :])
                            if t % 2:
                                last.then_inc(s["back"], 1)

                    for step in order:
                        name, u, k = step
                        if step in free:
                            sem, value = free[step]
                            pe.wait_ge(s[sem], value)
                        if name == "queries":
                            queries(u, pair[step])
                            if u == 0:
                                latents_by_token()
                        elif name == "scores":
                            scores(u, k, pair[step])
                        elif name == "turn":
                            turn(u, k)
                        elif name == "weigh":
                            weigh(u, k)
                        elif name == "spread":
                            spread(u)
                        elif name == "wout":
                            wout(u, pair[step])
                        elif name == "back":
                            back(u, pair[step])

                @block.scalar
                def _(act):
                    for c in range(NC):
                        act.wait_ge(s[f"xn_in{c}"], 16)
                        for k in range(KD):
                            act.activation(xnh[:, k, chunk(c)], xn[:, k, chunk(c)], ACT.Copy).then_inc(s["xhi"], 1)
                    act.wait_ge(s["f_in"], 16)
                    act.activation(fT[:, :, :], fT[:, :, :], ACT.Silu).then_inc(s["silu"], 1)
                    for c in range(NC):
                        act.wait_ge(s["lat"], c + 1)
                        act.activation(lath[:, chunk(c)], ps[:, 4 + c, :], ACT.Copy).then_inc(s["lathi"], 1)
                        act.activation(latf[:, chunk(c)], ps[0:DH, 4 + c, :], ACT.Copy).then_inc(s["latf"], 1)

                    def latents_by_token():
                        act.wait_ge(s["vt"], 1)
                        act.activation(latV[:, :, :], ps[:, 6, :].rearrange("p (t n) -> p t n", t=NT), ACT.Copy
                                       ).then_inc(s["v"], 1)

                    def queries(n, bank):
                        for i in range(2):
                            act.wait_ge(s["q"], 2 * n + i + 1)
                            if n >= UQ:
                                act.wait_ge(s["sc"], 4 * TC * (n - UQ + 1))
                            for a in range(2):
                                rows = slice(64 * a, 64 * a + 64)
                                act.activation(qst[rows, 2 * (2 * (n % UQ) + i) + a, :], ps[rows, bank + i, :], ACT.Copy
                                               ).then_inc(s["qhi"], 1)

                    def exps(u, h):
                        n = P * tiles_of(u)
                        act.wait_ge(s["ttr"], 4 * u + h + 1)
                        if h == 0 and u >= 3:
                            act.wait_ge(s["rl"], u - 2)
                        act.activation(SP[:, u % 3, h, 0:n], SP[:, u % 3, h, 0:n], ACT.Exp, bias=mn[:, u % 3, h:h + 1],
                                       scale=-1.0, accum_out=ls[:, u % 3, h:h + 1]).then_inc(s["ex"], 1)

                    def copy(u, k):
                        n = first[u] + k
                        if n % 2:
                            act.wait_ge(s["tr"], n + 1)
                            if n >= 4:
                                act.wait_ge(s["pv"], n - 3)
                            act.activation(PT[:, n % 4, :], ps[:, BT + n % NB, :], ACT.Copy).then_inc(s["eva"], 1)

                    def copy_r(u):
                        act.wait_ge(s["rb"], u + 1)
                        if u >= 2:
                            act.wait_ge(s["ctx"], u - 1)
                        act.activation(rbs[:, u % 2, :], ps[:, BC, 2 * P:4 * P], ACT.Copy).then_inc(s["rbs"], 1)

                    for step in order:
                        name, u, k = step
                        if name == "queries":
                            queries(u, pair[step])
                            if u == 0:
                                latents_by_token()
                        elif name == "scores":
                            exps(u, k)
                        elif name == "turn":
                            copy(u, k)
                        elif name == "spread":
                            copy_r(u)

                @block.vector
                def _(dve):
                    for c in range(NC):
                        for k in range(KD):
                            dve.wait_ge(s["xhi"], KD * c + k + 1)
                            dve.tensor_tensor(xnl[:, k, chunk(c)], xn[:, k, chunk(c)], xnh[:, k, chunk(c)],
                                              ALU.subtract).then_inc(s["xlo"], 1)
                    for c in range(NC):
                        dve.wait_ge(s["latf"], c + 1)
                        dve.tensor_tensor(latl[:, chunk(c)], ps[:, 4 + c, :], lath[:, chunk(c)], ALU.subtract
                                          ).then_inc(s["latlo"], 1)

                    def queries(n, bank):
                        for i in range(2):
                            for a in range(2):
                                here, there = slice(64 * a, 64 * a + 64), slice(64 - 64 * a, 128 - 64 * a)
                                head = 2 * (2 * (n % UQ) + i) + a
                                dve.wait_ge(s["qhi"], 4 * n + 2 * i + 2)
                                dve.tensor_tensor(qst[there, head, :], ps[here, bank + i, :], qst[here, head, :],
                                                  ALU.subtract).then_inc(s["qlo"], 1)

                    def masked(u, h, bank):
                        n = P * tiles_of(u)
                        dve.wait_ge(s["sc"], 4 * u + h + 1)
                        if h == 0 and u >= 3:
                            dve.wait_ge(s["tr"], first[u - 2])
                        src = ps[:, bank:bank + 2, :].rearrange("p a b -> p (a b)")[:, 0:n]
                        dve.tensor_tensor_reduce(SP[:, u % 3, h, 0:n], src, mask[:, N - n:N], -1.0, BIG, ALU.add,
                                                 ALU.min, mn[:, u % 3, h:h + 1]).then_inc(s["ttr"], 1)

                    def recip(u):
                        dve.wait_ge(s["ex"], 4 * (u + 1))
                        if u >= 2:
                            dve.wait_ge(s["rb"], u - 1)
                        dve.reciprocal(rl[:, u % 2, :], ls[:, u % 3, :]).then_inc(s["rl"], 1)

                    def copy(u, k):
                        n = first[u] + k
                        if n % 2 == 0:
                            dve.wait_ge(s["tr"], n + 1)
                            if n >= 4:
                                dve.wait_ge(s["pv"], n - 3)
                            dve.tensor_copy(PT[:, n % 4, :], ps[:, BT + n % NB, :]).then_inc(s["evd"], 1)

                    def normalise(u):
                        dve.wait_ge(s["pv"], first[u + 1])
                        dve.wait_ge(s["rbs"], u + 1)
                        if u >= 2:
                            dve.wait_ge(s["clo"], u - 1)
                        if u and u % UC == 0:
                            dve.wait_ge(s["wo"], KD * (u // UC))
                        dve.tensor_tensor(ctxf[:, u % 2, :], ps[:, BC, 0:2 * P], rbs[:, u % 2, :], ALU.mult
                                          ).then_inc(s["ctx"], 1)
                        dve.wait_ge(s["ctx"], u + 1)
                        j, t = 2 * (u // TC % UQ), u % TC
                        dve.tensor_copy(ch[:, j:j + 2, t * P:(t + 1) * P],
                                        ctxf[:, u % 2, :].rearrange("p (j k) -> p j k", j=2)).then_inc(s["chi"], 1)

                    def gate(c, bank):
                        dve.wait_ge(s["silu"], 1)
                        for m in range(KD):
                            dve.wait_ge(s["wo"], KD * c + m + 1)
                            dve.tensor_tensor(fT[:, m, chunk(c)], ps[:, bank + m, :], fT[:, m, chunk(c)], ALU.mult
                                              ).then_inc(s["prod"], 1)

                    def residual(c, bank):
                        dve.wait_ge(s["x_in"], 16)
                        for i in range(2):
                            dve.wait_ge(s["back"], 2 * c + i + 1)
                            rows = xtok[:, c * TC + 2 * i:c * TC + 2 * i + 2, :]
                            dve.tensor_tensor(rows, ps[:, bank + i, :].rearrange("p (t d) -> p t d", t=2), rows, ALU.add
                                              ).then_inc(s["y"], 1)

                    for step in order:
                        name, u, k = step
                        if name == "queries":
                            queries(u, pair[step])
                        elif name == "scores":
                            masked(u, k, pair[step])
                        elif name == "turn":
                            if k == 0:
                                recip(u)
                            copy(u, k)
                        elif name == "finish":
                            normalise(u)
                        elif name == "wout":
                            gate(u, pair[step])
                        elif name == "back":
                            residual(u, pair[step])

                @block.gpsimd
                def _(pool):
                    for u in range(UU):
                        pool.wait_ge(s["chi"], u + 1)
                        j, t = 2 * (u // TC % UQ), u % TC
                        cols = slice(t * P, (t + 1) * P)
                        pool.tensor_tensor(cl[:, j:j + 2, cols], ctxf[:, u % 2, :].rearrange("p (j k) -> p j k", j=2),
                                           ch[:, j:j + 2, cols], ALU.subtract).then_inc(s["clo"], 1)
            clear(nc, s)


def build(nc, x, Wq, Wkv_down, Wk_up, Wv_up, Wout, wqkv, q_scale, k_scale, wo, ln_g, ln_b, w1, b1, w2, b2,
          rot, out):
    xnorm = nc.dram_tensor("xnorm", [B, P, KD, N], F32).ap()
    state = nc.dram_tensor("state", [B, P, KD, N], F32).ap()
    with ExitStack() as ctx:
        ident = ctx.enter_context(nc.sbuf_tensor("ident", [P, P], F32))
        ones = ctx.enter_context(nc.sbuf_tensor("ones", [P, P], F32))
        eps = ctx.enter_context(nc.sbuf_tensor("eps", [P, 1], F32))
        ps = ctx.enter_context(nc.psum_tensor("ps", [P, 8, CH], F32))
        setup(nc, ident, ones, eps, semaphores(nc, ctx, "s_", "const"))
        stage_n(nc, x, xnorm, state, ident, eps, ps)
        stage_l(nc, (wqkv, q_scale, k_scale, wo, ln_g, ln_b, w1, b1, w2, b2, rot), state, ident, ones, eps, ps)
        stage_g(nc, x, (Wq, Wkv_down, Wk_up, Wv_up, Wout), xnorm, state, out, ident, ps)


_INS = ["L0_attn_x_bld", "L0_attn_Wq", "L0_attn_Wkv_down", "L0_attn_Wk_up", "L0_attn_Wv_up", "L0_attn_Wout",
        "L0_ffn_wqkv", "L0_ffn_q_scale", "L0_ffn_k_scale", "L0_ffn_wo", "L0_ffn_ln_g", "L0_ffn_ln_b",
        "L0_ffn_w1", "L0_ffn_b1", "L0_ffn_w2", "L0_ffn_b2"]


def kernel(**inputs):
    import numpy as _np
    import concourse.bacc as _bacc
    from concourse import mybir as _mybir
    from concourse.bass_utils import run_bass_kernel_spmd as _run

    nc = _bacc.Bacc("TRN2", target_bir_lowering=False, num_devices=1)
    arrays, args = {}, []
    for name in _INS:
        a = _np.ascontiguousarray(inputs[name])
        arrays[f"in_{name}_dram"] = a
        args.append(nc.dram_tensor(f"in_{name}_dram", a.shape, _mybir.dt.from_np(a.dtype), kind="ExternalInput").ap())
    rot = rotary_tables()
    arrays["rotary_dram"] = rot
    args.append(nc.dram_tensor("rotary_dram", rot.shape, _mybir.dt.from_np(rot.dtype), kind="ExternalInput").ap())
    args.append(nc.dram_tensor("out_0_dram", (B, N, D), _mybir.dt.float32, kind="ExternalOutput").ap())
    build(nc, *args)
    r = _run(nc, [arrays], core_ids=[0])
    return r.results[0]["out_0_dram"]
```
